# Optimizing a Trainium2 kernel written in Bass

```python
import numpy as np
import jax
import jax.numpy as jnp

def _softmax(x, axis=-1):
    return jax.nn.softmax(x, axis=axis)

def _gelu(x):
    return jax.nn.gelu(x, approximate=True)

def _silu(x):
    return jax.nn.silu(x)

def _sigmoid(x):
    return jax.nn.sigmoid(x)

def _layernorm(x, axis=-1, eps=1e-05):
    m = jnp.mean(x, axis=axis, keepdims=True)
    v = jnp.var(x, axis=axis, keepdims=True)
    return (x - m) / jnp.sqrt(v + eps)

def _scatter_add(tgt, idx, src, axis=0):
    return tgt.at[idx].add(src)

def _segment_sum(src, seg, n):
    return jax.ops.segment_sum(src, seg, n)
kernel_name = 'mk_xattn_ffn_d2_seqx_r8_f75c7f'

def setup_inputs(seed: int=0):
    np.random.seed(seed)
    _w = jnp.asarray

    def _rec_inputs():
        import jax
        import jax.numpy as jnp
        _rk = jax.random.key(seed)
        x = -0.0003929 + 0.9999 * jax.random.normal(jax.random.fold_in(_rk, 1), (128, 64, 128), jnp.float32)
        _lenS = 64 - jax.random.randint(jax.random.fold_in(_rk, 7), (128,), 0, max(1, 64 // 4) + 1, jnp.int32)
        _lenS2 = 64 - jax.random.randint(jax.random.fold_in(_rk, 8), (128,), 0, max(1, 64 // 4) + 1, jnp.int32)
        _ctx_1024P = jax.random.normal(jax.random.fold_in(_rk, 11), (128, 16, 128), jnp.float32)
        _ctx_1024c = jax.random.dirichlet(jax.random.fold_in(_rk, 511), 0.3 * jnp.ones((16,), jnp.float32), (128, 64))
        _ctx_1024t = jnp.einsum('bsk,bkd->bsd', _ctx_1024c, _ctx_1024P)
        _ctx_1024t = _ctx_1024t * jax.lax.rsqrt(jnp.mean(jnp.square(_ctx_1024t)) + 1e-12) * 0.953939
        ctx_1024 = 2.81802e-05 + 1.00001 * (_ctx_1024t + 0.3 * jax.random.normal(jax.random.fold_in(_rk, 611), (128, 64, 128), jnp.float32))
        _validS = jnp.arange(64)[None, :] < _lenS[:, None]
        _validS2 = jnp.arange(64)[None, :] < _lenS2[:, None]
        _causal = jnp.tril(jnp.ones((64, 64), dtype=bool))
        mask_BxS2_bf1 = jnp.ones((128, 64), dtype=bool)
        return (x, ctx_1024, mask_BxS2_bf1)
    x, ctx_1024, mask_BxS2_bf1 = _rec_inputs()

    def _L0_xattn_setup():
        import jax, jax.numpy as jnp
        import numpy as np
        D = 128
        key = jax.random.key(seed)
        ks = jax.random.split(key, 9)
        B, Nq, Nk = (8, 256, 256)
        s = 1.0 / np.sqrt(D)
        return {'query': jax.random.normal(ks[0], (B, Nq, D), jnp.float32), 'key': jax.random.normal(ks[1], (B, Nk, D), jnp.float32), 'value': jax.random.normal(ks[2], (B, Nk, D), jnp.float32), 'Wq': jax.random.uniform(ks[3], (D, D), jnp.float32, -s, s), 'bq': jax.random.uniform(ks[4], (D,), jnp.float32, -s, s), 'Wk': jax.random.uniform(ks[5], (D, D), jnp.float32, -s, s), 'bk': jax.random.uniform(ks[6], (D,), jnp.float32, -s, s), 'Wv': jax.random.uniform(ks[7], (D, D), jnp.float32, -s, s), 'bv': jax.random.uniform(ks[8], (D,), jnp.float32, -s, s)}
    _L0_xattn_all = _L0_xattn_setup()
    _L0_xattn_in = {k: v for k, v in _L0_xattn_all.items() if k in ('Wq', 'bq', 'Wk', 'bk', 'Wv', 'bv')}
    del _L0_xattn_all

    def _L0_ffn_setup():
        import jax, jax.numpy as jnp
        import numpy as np
        B, T, D = (4, 256, 128)
        H, DH, E, SEL = (8, 64, 5, 2)

        def _topk_mask(logits, k):
            _, idx = jax.lax.top_k(logits, k)
            return jnp.sum(jax.nn.one_hot(idx, logits.shape[-1], dtype=logits.dtype), axis=-2)
        key = jax.random.key(seed)
        ks = jax.random.split(key, 7)
        s = 0.02
        x = jax.random.normal(ks[0], (B, T, D), dtype=jnp.float32)
        Wq = jax.random.normal(ks[1], (D, H * DH), dtype=jnp.float32) * s
        Wk = jax.random.normal(ks[2], (D, H * DH), dtype=jnp.float32) * s
        Ws = jax.random.normal(ks[3], (D, H * E), dtype=jnp.float32) * s
        Wd = jax.random.normal(ks[4], (D, H * E), dtype=jnp.float32) * s
        Wv = jax.random.normal(ks[5], (E, D, DH), dtype=jnp.float32) * s
        Wo = jax.random.normal(ks[6], (E, DH, D), dtype=jnp.float32) * s
        return {'x': x, 'Wq': Wq, 'Wk': Wk, 'Ws': Ws, 'Wd': Wd, 'Wv': Wv, 'Wo': Wo}
    _L0_ffn_all = _L0_ffn_setup()
    _L0_ffn_in = {k: v for k, v in _L0_ffn_all.items() if k in ('Wq', 'Wk', 'Ws', 'Wd', 'Wv', 'Wo')}
    del _L0_ffn_all

    def _L1_xattn_setup():
        import jax, jax.numpy as jnp
        import numpy as np
        N_HEADS = 16
        D_MODEL = 128
        HEAD_DIM = D_MODEL // N_HEADS
        MASK_FILL = -100000000.0

        def _split_heads(x):
            B, S, _ = x.shape
            return x.reshape(B, S, N_HEADS, HEAD_DIM).transpose(0, 2, 1, 3)
        key = jax.random.key(seed)
        ks = jax.random.split(key, 12)
        B, L, P = (2, 256, 256)
        s = 1.0 / np.sqrt(D_MODEL).astype(np.float32)
        inp = {'q': jax.random.normal(ks[0], (B, L, D_MODEL), dtype=jnp.float32), 'k': jax.random.normal(ks[1], (B, P, D_MODEL), dtype=jnp.float32), 'v': jax.random.normal(ks[2], (B, P, D_MODEL), dtype=jnp.float32), 'attention_mask': jnp.ones((B, P), dtype=bool), 'Wq': jax.random.normal(ks[3], (D_MODEL, D_MODEL), dtype=jnp.float32) * s, 'bq': jnp.zeros((D_MODEL,), dtype=jnp.float32), 'Wk': jax.random.normal(ks[4], (D_MODEL, D_MODEL), dtype=jnp.float32) * s, 'bk': jnp.zeros((D_MODEL,), dtype=jnp.float32), 'Wv': jax.random.normal(ks[5], (D_MODEL, D_MODEL), dtype=jnp.float32) * s, 'bv': jnp.zeros((D_MODEL,), dtype=jnp.float32), 'Wo': jax.random.normal(ks[6], (D_MODEL, D_MODEL), dtype=jnp.float32) * s, 'bo': jnp.zeros((D_MODEL,), dtype=jnp.float32)}
        return inp
    _L1_xattn_all = _L1_xattn_setup()
    _L1_xattn_in = {k: v for k, v in _L1_xattn_all.items() if k in ('Wq', 'bq', 'Wk', 'bk', 'Wv', 'bv', 'Wo', 'bo')}
    del _L1_xattn_all

    def _L1_ffn_setup():
        import jax, jax.numpy as jnp
        import numpy as np
        B, S, D_MODEL, D_HIDDEN = (4, 256, 128, 512)

        def act_quant(x):
            scale = 127.0 / jnp.clip(jnp.max(jnp.abs(x), axis=-1, keepdims=True), 1e-05)
            return jnp.clip(jnp.round(x * scale), -128, 127) / scale

        def weight_quant(w):
            scale = 1.0 / jnp.clip(jnp.mean(jnp.abs(w)), 1e-05)
            return jnp.clip(jnp.round(w * scale), -1, 1) / scale

        def bit_linear(x, w):
            xq = x + jax.lax.stop_gradient(act_quant(x) - x)
            wq = w + jax.lax.stop_gradient(weight_quant(w) - w)
            return jnp.einsum('bsd,hd->bsh', xq, wq)

        def depthwise_conv1d(x_bcl, w, b):
            y = jax.lax.conv_general_dilated(x_bcl, w, window_strides=(1,), padding=[(1, 1)], dimension_numbers=('NCH', 'OIH', 'NCH'), feature_group_count=x_bcl.shape[1])
            return y + b[None, :, None]
        key = jax.random.key(seed)
        ks = jax.random.split(key, 5)
        lim1 = 1.0 / np.sqrt(D_MODEL)
        lim2 = 1.0 / np.sqrt(D_HIDDEN)
        limc = 1.0 / np.sqrt(3.0)
        return {'x': jax.random.normal(ks[0], (B, S, D_MODEL), dtype=jnp.float32), 'w1': jax.random.uniform(ks[1], (D_HIDDEN, D_MODEL), jnp.float32, -lim1, lim1), 'conv_w': jax.random.uniform(ks[2], (D_HIDDEN, 1, 3), jnp.float32, -limc, limc), 'conv_b': jax.random.uniform(ks[3], (D_HIDDEN,), jnp.float32, -limc, limc), 'w2': jax.random.uniform(ks[4], (D_MODEL, D_HIDDEN), jnp.float32, -lim2, lim2)}
    _L1_ffn_all = _L1_ffn_setup()
    _L1_ffn_in = {k: v for k, v in _L1_ffn_all.items() if k in ('w1', 'conv_w', 'conv_b', 'w2')}
    del _L1_ffn_all
    return {'x': x, 'ctx_1024': ctx_1024, 'mask_BxS2_bf1': mask_BxS2_bf1, 'L0_xattn_Wq': _L0_xattn_in['Wq'], 'L0_xattn_bq': _L0_xattn_in['bq'], 'L0_xattn_Wk': _L0_xattn_in['Wk'], 'L0_xattn_bk': _L0_xattn_in['bk'], 'L0_xattn_Wv': _L0_xattn_in['Wv'], 'L0_xattn_bv': _L0_xattn_in['bv'], 'L0_ffn_Wq': _L0_ffn_in['Wq'], 'L0_ffn_Wk': _L0_ffn_in['Wk'], 'L0_ffn_Ws': _L0_ffn_in['Ws'], 'L0_ffn_Wd': _L0_ffn_in['Wd'], 'L0_ffn_Wv': _L0_ffn_in['Wv'], 'L0_ffn_Wo': _L0_ffn_in['Wo'], 'L1_xattn_Wq': _L1_xattn_in['Wq'], 'L1_xattn_bq': _L1_xattn_in['bq'], 'L1_xattn_Wk': _L1_xattn_in['Wk'], 'L1_xattn_bk': _L1_xattn_in['bk'], 'L1_xattn_Wv': _L1_xattn_in['Wv'], 'L1_xattn_bv': _L1_xattn_in['bv'], 'L1_xattn_Wo': _L1_xattn_in['Wo'], 'L1_xattn_bo': _L1_xattn_in['bo'], 'L1_ffn_w1': _L1_ffn_in['w1'], 'L1_ffn_conv_w': _L1_ffn_in['conv_w'], 'L1_ffn_conv_b': _L1_ffn_in['conv_b'], 'L1_ffn_w2': _L1_ffn_in['w2']}

def reference(x, ctx_1024, mask_BxS2_bf1, L0_xattn_Wq, L0_xattn_bq, L0_xattn_Wk, L0_xattn_bk, L0_xattn_Wv, L0_xattn_bv, L0_ffn_Wq, L0_ffn_Wk, L0_ffn_Ws, L0_ffn_Wd, L0_ffn_Wv, L0_ffn_Wo, L1_xattn_Wq, L1_xattn_bq, L1_xattn_Wk, L1_xattn_bk, L1_xattn_Wv, L1_xattn_bv, L1_xattn_Wo, L1_xattn_bo, L1_ffn_w1, L1_ffn_conv_w, L1_ffn_conv_b, L1_ffn_w2):
    import jax
    import jax.numpy as jnp

    def _L0_xattn_ref(query, key, value, Wq, bq, Wk, bk, Wv, bv):
        import jax, jax.numpy as jnp
        import numpy as np
        D = 128
        q = jnp.einsum('bnd,ed->bne', query, Wq) + bq
        k = jnp.einsum('bnd,ed->bne', key, Wk) + bk
        v = jnp.einsum('bnd,ed->bne', value, Wv) + bv
        scores = jnp.einsum('bqd,bkd->bqk', q, k)
        attn = jax.nn.softmax(scores, axis=-1)
        return jnp.einsum('bqk,bkd->bqd', attn, v)

    def _L0_ffn_ref(x, Wq, Wk, Ws, Wd, Wv, Wo):
        import jax, jax.numpy as jnp
        import numpy as np
        B, T, D = (4, 256, 128)
        H, DH, E, SEL = (8, 64, 5, 2)

        def _topk_mask(logits, k):
            _, idx = jax.lax.top_k(logits, k)
            return jnp.sum(jax.nn.one_hot(idx, logits.shape[-1], dtype=logits.dtype), axis=-2)
        e, d, dh = Wv.shape
        h = Wq.shape[1] // dh
        b, t, _ = x.shape
        scale = dh ** (-0.5)
        q = (x @ Wq).reshape(b, t, h, dh).transpose(0, 2, 1, 3)
        k = (x @ Wk).reshape(b, t, h, dh).transpose(0, 2, 1, 3)
        gl_v = (x @ Ws).reshape(b, t, h, e)
        wv = _topk_mask(gl_v, SEL) * jax.nn.sigmoid(gl_v)
        xv = jnp.einsum('btd,edk->btek', x, Wv)
        v = jnp.einsum('bthe,btek->bhtk', wv, xv)
        scores = jnp.einsum('bhid,bhjd->bhij', q * scale, k)
        probs = jax.nn.softmax(scores, axis=-1)
        attn = jnp.einsum('bhij,bhjd->bihd', probs, v)
        gl_o = (x @ Wd).reshape(b, t, h, e)
        mask_o = _topk_mask(gl_o, SEL)
        out = jnp.einsum('bthe,bthk,ekd->btd', mask_o, attn, Wo)
        return out

    def _L1_xattn_ref(q, k, v, attention_mask, Wq, bq, Wk, bk, Wv, bv, Wo, bo):
        import jax, jax.numpy as jnp
        import numpy as np
        N_HEADS = 16
        D_MODEL = 128
        HEAD_DIM = D_MODEL // N_HEADS
        MASK_FILL = -100000000.0

        def _split_heads(x):
            B, S, _ = x.shape
            return x.reshape(B, S, N_HEADS, HEAD_DIM).transpose(0, 2, 1, 3)
        qm = _split_heads(q @ Wq.T + bq)
        km = _split_heads(k @ Wk.T + bk)
        vm = _split_heads(v @ Wv.T + bv)
        scores = jnp.einsum('bnlh,bnph->bnlp', qm, km) / np.sqrt(HEAD_DIM).astype(np.float32)
        mask = attention_mask[:, None, None, :]
        scores = jnp.where(mask, scores, MASK_FILL)
        attn = jax.nn.softmax(scores, axis=-1)
        out = jnp.einsum('bnlp,bnph->bnlh', attn, vm)
        B, _, L, _ = out.shape
        out = out.transpose(0, 2, 1, 3).reshape(B, L, D_MODEL)
        return out @ Wo.T + bo

    def _L1_ffn_ref(x, w1, conv_w, conv_b, w2):
        import jax, jax.numpy as jnp
        import numpy as np
        B, S, D_MODEL, D_HIDDEN = (4, 256, 128, 512)

        def act_quant(x):
            scale = 127.0 / jnp.clip(jnp.max(jnp.abs(x), axis=-1, keepdims=True), 1e-05)
            return jnp.clip(jnp.round(x * scale), -128, 127) / scale

        def weight_quant(w):
            scale = 1.0 / jnp.clip(jnp.mean(jnp.abs(w)), 1e-05)
            return jnp.clip(jnp.round(w * scale), -1, 1) / scale

        def bit_linear(x, w):
            xq = x + jax.lax.stop_gradient(act_quant(x) - x)
            wq = w + jax.lax.stop_gradient(weight_quant(w) - w)
            return jnp.einsum('bsd,hd->bsh', xq, wq)

        def depthwise_conv1d(x_bcl, w, b):
            y = jax.lax.conv_general_dilated(x_bcl, w, window_strides=(1,), padding=[(1, 1)], dimension_numbers=('NCH', 'OIH', 'NCH'), feature_group_count=x_bcl.shape[1])
            return y + b[None, :, None]
        h = bit_linear(x, w1)
        h = depthwise_conv1d(h.transpose(0, 2, 1), conv_w, conv_b)
        h = h.transpose(0, 2, 1)
        h = jax.nn.silu(h)
        return bit_linear(h, w2)
    x = x + _L0_xattn_ref(_layernorm(x, axis=-1), ctx_1024, ctx_1024, L0_xattn_Wq, L0_xattn_bq, L0_xattn_Wk, L0_xattn_bk, L0_xattn_Wv, L0_xattn_bv)
    x = x + _L0_ffn_ref(_layernorm(x, axis=-1), L0_ffn_Wq, L0_ffn_Wk, L0_ffn_Ws, L0_ffn_Wd, L0_ffn_Wv, L0_ffn_Wo)
    x = x + _L1_xattn_ref(_layernorm(x, axis=-1), ctx_1024, ctx_1024, mask_BxS2_bf1, L1_xattn_Wq, L1_xattn_bq, L1_xattn_Wk, L1_xattn_bk, L1_xattn_Wv, L1_xattn_bv, L1_xattn_Wo, L1_xattn_bo)
    x = x + _L1_ffn_ref(_layernorm(x, axis=-1), L1_ffn_w1, L1_ffn_conv_w, L1_ffn_conv_b, L1_ffn_w2)
    return x

_drawn_inputs = setup_inputs


def setup_inputs(seed=0):
    import zlib

    import numpy as np

    out = dict(_drawn_inputs(seed))
    spreads = {'L1_xattn_bq': (0.0, 0.41),
     'L1_xattn_bk': (0.0, 0.8),
     'L1_xattn_bv': (0.0, 0.1),
     'L1_xattn_bo': (0.0, 0.1)}
    factors = {'L0_xattn_bk': 8.0,
     'L0_ffn_Wq': 8.0,
     'L0_ffn_Wk': 8.0,
     'L0_ffn_Ws': 4.912,
     'L0_ffn_Wd': 3.479}
    for name, (base, spread) in spreads.items():
        noise = np.random.default_rng([zlib.crc32(name.encode()), seed]).standard_normal(out[name].shape)
        drawn = base * np.exp(spread * noise) if base else spread * noise
        out[name] = jnp.asarray(drawn.astype(out[name].dtype))
    for name, factor in factors.items():
        out[name] = (out[name] * factor).astype(out[name].dtype)
    return out
```

```python
from contextlib import ExitStack

import concourse.bass as bass
from concourse import mybir

F32 = mybir.dt.float32
BF16 = mybir.dt.bfloat16
U8 = mybir.dt.uint8
ALU = mybir.AluOpType
ACT = mybir.ActivationFunctionType
AX = mybir.AxisListType.X

P = 128
NB, SEQ, D = 128, 64, 128
TOK = P
TILES = NB * SEQ // TOK
LN_EPS = 1e-5
H0, DH, E = 8, 64, 5
J0 = H0 // 2
NG = H0 * E
XV = E * DH
ZW = 384
H1, HD = 16, 8
J1 = H1 // 2
VW = HD + 1
MASK_BIG = float(2 ** 28)
CROSS = -1e30
HID, TAPS = 512, 3
HC = HID // P
ROUND = float(1.5 * 2 ** 23)
QMAX, QMIN, QCLIP = 127.0, -128.0, 1e-5

LAG = {"load": -2, "stat": -1, "attn0": 0, "moe": 1, "mix": 2, "ctx1": 2, "attn1": 3, "ffn": 4}
FIRST, LAST = -2, TILES - 1 + 4
LOOP_FROM, LOOP_TO = 6, TILES - 2
SETUP_SUMS, SETUP_Q = 3, 22
SETUP_V = SETUP_Q + TAPS * HC + TAPS + 2

EVENTS = """x_stats x_rstd x1_stats x1_rstd x2_stats x2_rstd x3_stats x3_rstd
 a_mean a_xn a_T a_XT a_qkv a_q a_k a_v a_S a_max a_P a_recip a_PT a_PTs a_O a_x1 a_xb
 x_bn x1_bn x2_bn x3_bn x_var x1_var x2_var x3_var
 b_xn b_T b_XT b_gx b_q b_k b_GX b_Q0 b_Q1 b_K b_th b_cmp b_rank b_mask b_wv b_VP b_v1 b_v2 b_V
 b_S b_max b_sub b_PT b_P b_O b_OS0 b_OS1 b_recip b_cf
 z_ZP z_1 z_2 z_Z z_T z_ZT z_out z_x2
 c_xn c_T c_XT c_qkv c_Q0 c_Q1 c_K c_V0 c_V1 c_mf c_KM1 c_KM c_ng c_S0 c_S1 c_max0 c_sub0 c_max1 c_sub1
 c_PT0 c_PT1 c_P0 c_P1 c_O c_r0 c_r1 c_n0 c_n1 c_OT c_OTs c_out c_x3 c_xb
 d_xn d_am d_cl d_rc d_sc d_rs d_q1 d_q2 d_q3 d_T d_XP d_y d_th d_g d_gam d_gcl d_grc d_gsc d_grs d_g1 d_g2
 d_GT d_GTs d_acc d_out""".split()


def moe_transformer(nc, x, ctx1024, mask, w, consts, out):
    x_rows = x.rearrange("b s d -> (b s) d")
    ctx_rows = ctx1024.rearrange("b s d -> (b s) d")
    out_rows = out.rearrange("b s d -> (b s) d")
    mask_row = mask.rearrange("(o b) s -> o (b s)", o=1)

    with ExitStack() as ctx:
        def sb(name, shape, dt=F32):
            return ctx.enter_context(nc.sbuf_tensor(name, shape, dt))

        def sem(name):
            return ctx.enter_context(nc.semaphore(name))

        bank = [ctx.enter_context(nc.psum_tensor(f"bank{i}", [P, 512], F32)) for i in range(8)]
        bA, b0, b1, b2, c0, c1, d0, d1 = bank

        ident = sb("ident", [P, P])
        to_alternating, from_alternating = sb("to_alternating", [P, P]), sb("from_alternating", [P, P])
        halfneg = sb("halfneg", [P, 1])
        neground = sb("neground", [P, 1])
        ones = sb("ones", [P, P])
        onesb = sb("onesb", [P, P], BF16)
        jmask = sb("jmask", [P, J1])
        batch_f = sb("batch_f", [2, 2, P])
        batch_b = sb("batch_b", [2, 2, P], BF16)
        a_wq, a_wk, a_wv = sb("a_wq", [P, P]), sb("a_wk", [P, P]), sb("a_wv", [P, P])
        a_bq, a_bk, a_bv = sb("a_bq", [P, 1]), sb("a_bk", [P, 1]), sb("a_bv", [P, P])
        m_wq, m_wk = sb("m_wq", [P, 512]), sb("m_wk", [P, 512])
        m_wg = sb("m_wg", [P, 2 * NG + XV])
        m_wv = sb("m_wv", [P, XV])
        m_wo = sb("m_wo", [P, 3, P])
        c_wq, c_wk, c_wv = sb("c_wq", [P, P]), sb("c_wk", [P, P]), sb("c_wv", [P, P])
        c_bq, c_bk = sb("c_bq", [P, 1]), sb("c_bk", [P, 1])
        c_wo = sb("c_wo", [P, 2, P])
        c_woT, c_bv, c_bo = sb("c_woT", [P, P]), sb("c_bv", [P, 1]), sb("c_bo", [P, P])
        c_bvw = sb("c_bvw", [P, P])
        c_bias = sb("c_bias", [P, P])
        w1raw, w2raw = sb("w1raw", [P, HC, P]), sb("w2raw", [P, HID])
        w1q, w2q = sb("w1q", [P, HC, P]), sb("w2q", [P, HID])
        wstat = sb("wstat", [P, 12])
        convw = sb("convw", [P, HC, TAPS])
        w1taps = sb("w1taps", [P, TAPS, HC, P])
        W1K = sb("W1K", [P, TAPS, HID])
        W2T = sb("W2T", [P, HC, P], BF16)
        convb = sb("convb", [3, HID])
        cb_hi, cb_mid, cb_lo = (sb(n, [3, HID], BF16) for n in ("cb_hi", "cb_mid", "cb_lo"))
        cb_r1, cb_r2, cb_s1, cb_s2 = (sb(n, [3, HID]) for n in ("cb_r1", "cb_r2", "cb_s1", "cb_s2"))
        CB = sb("CB", [3, HID], BF16)

        xin = [sb(f"xin{i}", [P, D]) for i in range(2)]
        cin = [sb(f"cin{i}", [P, D]) for i in range(2)]
        cin1 = [sb(f"cin1_{i}", [P, D]) for i in range(2)]
        mrow = [sb(f"mrow{i}", [P, TOK], U8) for i in range(2)]
        x1 = [sb(f"x1_{i}", [P, D]) for i in range(2)]
        x2 = [sb(f"x2_{i}", [P, D]) for i in range(2)]
        x3 = [sb(f"x3_{i}", [P, D]) for i in range(2)]
        y = [sb(f"y{i}", [P, D]) for i in range(2)]
        stat = {s: [sb(f"st_{s}{i}", [P, 16]) for i in range(2)] for s in ("x", "x1", "x2", "x3")}

        a_xn, a_XT = sb("a_xn", [P, P]), sb("a_XT", [P, 2, P])
        a_Q, a_K, a_V, a_P, a_PT = (sb(n, [P, P]) for n in ("a_Q", "a_K", "a_V", "a_P", "a_PT"))
        a_small, a_xb = sb("a_small", [P, 4]), sb("a_xb", [P, P])

        b_xn, b_XT = sb("b_xn", [P, P]), sb("b_XT", [P, P])
        b_GX = sb("b_GX", [P, 2 * NG + XV])
        b_Q = sb("b_Q", [P, J0, 2, 2, SEQ])
        b_K = sb("b_K", [P, J0, TOK])
        b_th, b_wv = sb("b_th", [P, NG]), sb("b_wv", [P, NG])
        b_cmp = sb("b_cmp", [P, 2 * H0, E, E - 1])
        b_rank, b_mask = sb("b_rank", [P, 2 * NG]), sb("b_mask", [P, 2 * NG])
        b_VP = sb("b_VP", [P, E, H0 * DH])
        b_V1, b_V2 = sb("b_V1", [P, 2, H0 * DH]), sb("b_V2", [P, H0 * DH])
        b_V = sb("b_V", [P, H0, DH + 1])
        b_max, b_D, b_PT = sb("b_max", [P, 8]), sb("b_D", [P, 512]), sb("b_PT", [P, 512])
        b_O = sb("b_O", [P, H0, DH + 1])
        b_r, b_cf = sb("b_r", [P, H0]), sb("b_cf", [P, NG])
        z_P = sb("z_P", [P, H0, XV])
        z_1, z_2 = sb("z_1", [P, 4, XV]), sb("z_2", [P, 2, XV])
        z_Z, z_ZT = sb("z_Z", [P, ZW]), sb("z_ZT", [P, ZW])

        c_xn, c_XT = sb("c_xn", [P, P]), sb("c_XT", [P, 2, P])
        c_Q = sb("c_Q", [P, 2, 2, SEQ])
        c_K, c_KM1 = sb("c_K", [P, P]), sb("c_KM1", [P, P])
        c_KM = sb("c_KM", [P, J1, TOK])
        c_mf = sb("c_mf", [P, TOK])
        c_ng = sb("c_ng", [1, TOK], BF16)
        c_V = sb("c_V", [P, J1, 2, 2, VW])
        c_max, c_D, c_PT = sb("c_max", [P, 2, J1]), sb("c_D", [P, J1, 2, SEQ]), sb("c_PT", [P, J1 * P])
        c_r, c_ON, c_OT = sb("c_r", [P, J1, 2]), sb("c_ON", [P, 2, J1, HD]), sb("c_OT", [P, P])
        c_xb = sb("c_xb", [P, P])

        d_xn, d_q1, d_q2, d_q3 = (sb(n, [P, P]) for n in ("d_xn", "d_q1", "d_q2", "d_q3"))
        d_s = sb("d_s", [P, 16])
        d_XP = sb("d_XP", [P, (SEQ + 2) * 2])
        d_th, d_g, d_g1, d_g2 = (sb(n, [P, HID]) for n in ("d_th", "d_g", "d_g1", "d_g2"))
        d_GT = sb("d_GT", [P, HC, P], BF16)

        ev = {n: sem(n) for n in EVENTS}
        x_in = [sem("x_in0"), sem("x_in1")]
        c_in = [sem("c_in0"), sem("c_in1")]
        y_out = [sem("y_out0"), sem("y_out1")]
        passed = {"pe": sem("pe_passed"), "dve": sem("dve_passed")}
        w_in = sem("w_in")
        zeroed = sem("zeroed")
        setup_v, setup_t = sem("setup_v"), sem("setup_t")

        def need(eng, name, count):
            if not (isinstance(count, int) and count <= 0):
                eng.wait_ge(ev[name], count)

        def gate(eng, name):
            eng.sem_inc(passed[name], 1)

        def sig(ins, name):
            return ins.then_inc(ev[name], 1)

        def tile_dmas(t, i):
            if isinstance(t, int):
                return 32 * (t // 2 + 1)
            return (t - i) * 16 + 32

        def step(program, n, par):
            for stage, part in program:
                t = n - LAG[stage]
                if isinstance(n, int) and not 0 <= t < TILES:
                    continue
                part(t, (par + LAG[stage]) % 2)

        def run(eng, program):
            for n in range(FIRST, LOOP_FROM):
                step(program, n, n % 2)
            with eng.Fori(LOOP_FROM // 2, LOOP_TO // 2) as i:
                for par in range(2):
                    step(program, 2 * i + par, par)
            for n in range(LOOP_TO, LAST + 1):
                step(program, n, n % 2)

        weights = [(ident[:, :], consts["ident"]), (jmask[:, :], consts["jmask"]),
                   (to_alternating[:, :], consts["alt"]), (from_alternating[:, :], consts["altT"]),
                   (batch_f[:, :, :], consts["batch"]),
                   (a_wq[:, :], w["a_wqT"]), (a_wk[:, :], w["a_wkT"]), (a_wv[:, :], w["a_wvT"]),
                   (a_bq[:, :], w["a_bq"]), (a_bk[:, :], w["a_bk"]),
                   (a_bv[:, :], w["a_bv"].broadcast_to([P, P])),
                   (m_wq[:, :], w["m_wq"]), (m_wk[:, :], w["m_wk"]),
                   (m_wg[:, 0:NG], w["m_ws"]), (m_wg[:, NG:2 * NG], w["m_wd"]),
                   (m_wv[:, :].rearrange("d (e k) -> d e k", e=E), w["m_wv"].rearrange("e d k -> d e k")),
                   (m_wo[:, 0:2, :], w["m_wo"].rearrange("e k d -> (e k) d")[0:256, :].rearrange("(c p) d -> p c d", p=P)),
                   (m_wo[0:DH, 2, :], w["m_wo"].rearrange("e k d -> (e k) d")[256:320, :]),
                   (c_wq[:, :], w["c_wqT"]), (c_wk[:, :], w["c_wkT"]), (c_wv[:, :], w["c_wvT"]),
                   (c_bq[:, :], w["c_bq"]), (c_bk[:, :], w["c_bk"]), (c_bv[:, :], w["c_bv"]),
                   (c_bo[:, :], w["c_bo"].broadcast_to([P, P])), (c_woT[:, :], w["c_woT"]),
                   (c_wo[0:64, :, :], w["c_woT"].rearrange("(s r) e -> r s e", s=2)),
                   (c_wo[64:128, :, :], w["c_woT"].rearrange("(s r) e -> r s e", s=2)),
                   (w1raw[:, :, :], w["w1"].rearrange("(c p) d -> p c d", p=P)),
                   (convw[:, :, :], w["convw"].rearrange("(c p) o k -> p c (o k)", p=P)),
                   (convb[:, :], w["convb"].broadcast_to([3, HID])),
                   (w2raw[:, :], w["w2"])]

        block = ctx.enter_context(nc.Block())

        @block.sync
        def _(sp):
            for dst, src in weights:
                sp.dma_start(dst, src).then_inc(w_in, 16)

            def load(t, i):
                need(sp, "a_xn", t - 1)
                need(sp, "a_xb", t - 1)
                need(sp, "x_bn", t - 1)
                need(sp, "a_T", t - 1)
                sp.dma_start(xin[i][:, :], x_rows[bass.ds(t * TOK, TOK), :]).then_inc(x_in[i], 16)
                sp.dma_start(cin[i][:, :], ctx_rows[bass.ds(t * TOK, TOK), :]).then_inc(x_in[i], 16)

            def load1(t, i):
                need(sp, "c_T", t - 1)
                need(sp, "c_ng", t - 1)
                sp.dma_start(cin1[i][:, :], ctx_rows[bass.ds(t * TOK, TOK), :]).then_inc(c_in[i], 16)
                sp.dma_start(mrow[i][:, :], mask_row[:, bass.ds(t * TOK, TOK)].broadcast_to([P, TOK])).then_inc(c_in[i], 16)

            def store(t, i):
                need(sp, "d_out", t + 1)
                sp.dma_start(out_rows[bass.ds(t * TOK, TOK), :], y[i][:, :]).then_inc(y_out[i], 16)

            run(sp, [("load", load), ("ctx1", load1), ("ffn", store)])
            for i in range(2):
                sp.wait_ge(y_out[i], 16 * (TILES // 2))

        @block.gpsimd
        def _(pool):
            fills = ((b_Q[:, :, :, :, :], 0.0), (c_Q[:, :, :, :], 0.0), (c_V[:, :, :, :, :], 0.0),
                     (z_Z[:, XV:ZW], 0.0), (m_wo[DH:P, 2, :], 0.0), (d_XP[:, :], 0.0),
                     (b_V[:, :, DH:DH + 1], 1.0), (ones[:, :], 1.0), (onesb[:, :], 1.0),
                     (halfneg[:, :], -0.5), (neground[:, :], -ROUND),
                     *((c_V[64 * b:64 * b + 64, :, :, b, HD:VW], 1.0) for b in range(2)))
            for n, (ap, value) in enumerate(fills):
                nc.gpsimd.memset(ap, value).then_inc(zeroed, 1)
                pool.wait_ge(zeroed, n + 1)
            pool.wait_ge(w_in, 16 * len(weights))
            pool.wait_ge(setup_v, SETUP_V)

            def rstd(s):
                def part(t, i):
                    need(pool, s + "_var", t + 1)
                    sig(nc.gpsimd.tensor_tensor(stat[s][i][:, 9:10], stat[s][i][:, 8:9], halfneg[:, :], ALU.pow),
                        s + "_rstd")
                return part

            def a_bias(t, i):
                pool.wait_ge(x_in[i], tile_dmas(t, i))
                need(pool, "a_x1", t)
                sig(nc.gpsimd.tensor_tensor(a_xb[:, :], xin[i][:, :], a_bv[:, :], ALU.add), "a_xb")

            def b_vprod(t, i):
                need(pool, "b_wv", t + 1)
                need(pool, "b_GX", t + 1)
                need(pool, "b_V", t)
                o = b_VP[:, :, :].rearrange("p e (h k) -> p e h k", h=H0)
                g = b_wv[:, :].rearrange("p (h e) -> p e h", e=E).unsqueeze(3).broadcast_to([P, E, H0, DH])
                v = b_GX[:, 2 * NG:].rearrange("p (e k) -> p e k", e=E).unsqueeze(2).broadcast_to([P, E, H0, DH])
                sig(nc.gpsimd.tensor_tensor(o, g, v, ALU.mult), "b_VP")

            def z_prod(t, i):
                need(pool, "b_cf", t + 1)
                need(pool, "b_OS0", t + 1)
                need(pool, "b_OS1", t + 1)
                need(pool, "z_1", t)
                o = z_P[:, :, :].rearrange("p h (e k) -> p h e k", e=E)
                a = b_O[:, :, 0:DH].unsqueeze(2).broadcast_to([P, H0, E, DH])
                c = b_cf[:, :].rearrange("p (h e) -> p h e", e=E).unsqueeze(3).broadcast_to([P, H0, E, DH])
                sig(nc.gpsimd.tensor_tensor(o, a, c, ALU.mult), "z_ZP")

            def c_bias_add(t, i):
                need(pool, "z_x2", t + 1)
                need(pool, "c_x3", t)
                sig(nc.gpsimd.tensor_tensor(c_xb[:, :], x2[i][:, :], c_bias[:, :], ALU.add), "c_xb")

            def c_keys(t, i):
                need(pool, "c_K", t + 1)
                need(pool, "c_mf", t + 1)
                need(pool, "c_KM", t)
                sig(nc.gpsimd.tensor_tensor(c_KM1[:, :], c_K[:, :], c_mf[:, :], ALU.mult), "c_KM1")
                need(pool, "c_KM1", t + 1)
                need(pool, "c_S1", t)
                sig(nc.gpsimd.tensor_tensor(c_KM[:, :, :], c_KM1[:, :].unsqueeze(1).broadcast_to([P, J1, TOK]),
                                            jmask[:, :].unsqueeze(2).broadcast_to([P, J1, TOK]), ALU.mult), "c_KM")

            run(pool, [("attn0", a_bias), ("attn1", c_bias_add), ("attn1", c_keys),
                       ("mix", z_prod), ("moe", b_vprod),
                       ("stat", rstd("x")), ("mix", rstd("x2")), ("attn0", rstd("x1")), ("attn1", rstd("x3"))])

        @block.scalar
        def _(act):
            act.wait_ge(setup_v, SETUP_V)
            act.wait_ge(zeroed, 13)
            act.wait_ge(w_in, 16 * len(weights))

            def copy(o, i_, name):
                return sig(nc.scalar.activation(o, i_, ACT.Copy), name)

            def b_xt(t, i):
                need(act, "b_T", t + 1)
                need(act, "b_k", t)
                need(act, "b_gx", t)
                copy(b_XT[:, :], b0[:, 0:P], "b_XT")

            def c_xt(t, i):
                need(act, "c_T", t + 1)
                need(act, "c_qkv", t)
                copy(c_XT[:, :, :].rearrange("p a b -> p (a b)"), c0[:, 0:2 * P], "c_XT")

            def d_xt(t, i):
                need(act, "d_T", t + 1)
                need(act, "d_y", t)
                copy(d_XP[:, 2:2 + TOK], d0[:, 0:P], "d_XP")

            def a_xt(t, i):
                need(act, "a_T", t + 1)
                need(act, "a_qkv", t)
                copy(a_XT[:, :, :].rearrange("p a b -> p (a b)"), bA[:, 0:2 * P], "a_XT")

            def b_gxs(t, i):
                need(act, "b_gx", t + 1)
                need(act, "b_VP", t)
                need(act, "b_cmp", t)
                copy(b_GX[:, :], b2[:, 0:2 * NG + XV], "b_GX")
                need(act, "b_GX", t + 1)
                need(act, "b_wv", t)
                sig(nc.scalar.activation(b_th[:, :], b_GX[:, 0:NG], ACT.Tanh, scale=0.5), "b_th")

            def b_qk(t, i):
                need(act, "b_q", t + 1)
                need(act, "b_S", t)
                for hh in range(2):
                    rows = slice(64 * hh, 64 * hh + 64)
                    sig(nc.scalar.activation(b_Q[rows, :, :, hh, :],
                                             b0[rows, :].rearrange("p (j b q) -> p j b q", j=J0, b=2),
                                             ACT.Copy, scale=float(DH) ** -0.5), f"b_Q{hh}")
                need(act, "b_k", t + 1)
                copy(b_K[:, :, :].rearrange("p j s -> p (j s)"), b1[:, :], "b_K")

            def c_qkvs(t, i):
                need(act, "c_qkv", t + 1)
                need(act, "c_S1", t)
                for s in range(2):
                    rows = slice(64 * s, 64 * s + 64)
                    sig(nc.scalar.activation(c_Q[rows, :, s, :], c0[rows, 0:P].rearrange("p (b q) -> p b q", b=2),
                                             ACT.Identity, bias=c_bq[rows, :]), f"c_Q{s}")
                need(act, "c_KM1", t)
                sig(nc.scalar.activation(c_K[:, :], c0[:, P:2 * P], ACT.Identity, bias=c_bk[:, :]), "c_K")
                need(act, "c_O", t)
                for b in range(2):
                    rows = slice(64 * b, 64 * b + 64)
                    copy(c_V[rows, :, :, b, 0:HD].rearrange("p j s d -> p s j d"),
                         c0[rows, 2 * P:3 * P].rearrange("p (s j d) -> p s j d", s=2, j=J1), f"c_V{b}")

            def a_qkvs(t, i):
                need(act, "a_qkv", t + 1)
                need(act, "a_S", t)
                sig(nc.scalar.activation(a_Q[:, :], bA[:, 0:P], ACT.Identity, bias=a_bq[:, :]), "a_q")
                sig(nc.scalar.activation(a_K[:, :], bA[:, P:2 * P], ACT.Identity, bias=a_bk[:, :]), "a_k")
                need(act, "a_O", t)
                copy(a_V[:, :], bA[:, 2 * P:3 * P], "a_v")

            def d_tanh(t, i):
                need(act, "d_y", t + 1)
                need(act, "d_g", t)
                sig(nc.scalar.activation(d_th[:, :], d1[:, :], ACT.Tanh, scale=0.5), "d_th")

            def a_exp(t, i):
                need(act, "a_max", t + 1)
                need(act, "a_PT", t)
                need(act, "a_recip", t)
                sig(nc.scalar.activation(a_P[:, :], bA[:, 0:P], ACT.Exp, bias=a_small[:, 0:1],
                                         accum_out=a_small[:, 1:2]), "a_P")

            def b_exp(t, i):
                need(act, "b_PT", t + 1)
                need(act, "b_O", t)
                sig(nc.scalar.activation(b_PT[:, :], b1[:, :], ACT.Exp), "b_P")

            def a_pt(t, i):
                need(act, "a_PT", t + 1)
                need(act, "a_O", t)
                copy(a_PT[:, :], bA[:, P:2 * P], "a_PTs")

            def c_exp(t, i):
                need(act, "c_PT0", t + 1)
                need(act, "c_O", t)
                sig(nc.scalar.activation(c_PT[:, 0:512], c0[:, :], ACT.Exp, scale=float(HD) ** -0.5), "c_P0")
                need(act, "c_PT1", t + 1)
                sig(nc.scalar.activation(c_PT[:, 512:1024], c1[:, :], ACT.Exp, scale=float(HD) ** -0.5), "c_P1")

            def d_gt(t, i):
                need(act, "d_GT", t + 1)
                need(act, "d_acc", t)
                sig(nc.scalar.activation(d_GT[:, :, :].rearrange("p c s -> p (c s)"), d0[:, :], ACT.Identity,
                                         bias=neground[:, :]), "d_GTs")

            def z_t(t, i):
                need(act, "z_T", t + 1)
                need(act, "z_out", t)
                copy(z_ZT[:, :], b1[:, 0:ZW], "z_ZT")

            def b_os(t, i):
                need(act, "b_O", t + 1)
                need(act, "z_ZP", t)
                need(act, "b_recip", t)
                copy(b_O[:, 0:4, :].rearrange("p h k -> p (h k)"), b0[:, 0:4 * (DH + 1)], "b_OS0")
                copy(b_O[:, 4:8, :].rearrange("p h k -> p (h k)"), b2[:, 0:4 * (DH + 1)], "b_OS1")

            def c_ot(t, i):
                need(act, "c_OT", t + 1)
                need(act, "c_out", t)
                copy(c_OT[:, :], c1[:, 0:P], "c_OTs")

            run(act, [("moe", b_xt), ("attn1", c_xt), ("ffn", d_xt), ("attn0", a_xt),
                      ("moe", b_gxs), ("moe", b_qk), ("attn1", c_qkvs), ("attn0", a_qkvs), ("ffn", d_tanh),
                      ("attn0", a_exp), ("moe", b_exp), ("attn0", a_pt), ("attn1", c_exp), ("ffn", d_gt),
                      ("mix", z_t), ("attn1", c_ot), ("moe", b_os)])

        @block.tensor
        def _(pe):
            pe.wait_ge(w_in, 16 * len(weights))
            pe.wait_ge(zeroed, 13)
            pe.wait_ge(setup_v, SETUP_SUMS)
            nc.tensor.matmul(bA[:, 0:P], c_bvw[:, :], c_woT[:, :], start=True, stop=True).then_inc(setup_t, 1)
            nc.tensor.matmul(b0[:, 0:2], ones[:, :], wstat[:, 0:2], start=True, stop=True).then_inc(setup_t, 1)
            for k in range(TAPS):
                pe.wait_ge(setup_v, SETUP_Q + HC * (k + 1))
                for c in range(HC):
                    last = nc.tensor.transpose([b1, b2, c0][k][:, c * P:(c + 1) * P], w1taps[:, k, c, :], ident[:, :])
                last.then_inc(setup_t, 1)
            for c in range(HC):
                last = nc.tensor.transpose(c1[:, c * P:(c + 1) * P], w2q[:, c * P:(c + 1) * P], ident[:, :])
            last.then_inc(setup_t, 1)
            pe.wait_ge(setup_v, SETUP_V)

            def mm(o, l, r, start=True, stop=True):
                return nc.tensor.matmul(o, l, r, start=start, stop=stop)

            def turn(o, a, order=ident):
                return nc.tensor.transpose(o, a, order[:, :])

            def b_turn(t, i):
                need(pe, "b_xn", t + 1)
                need(pe, "b_OS0", t)
                sig(turn(b0[:, 0:P], b_xn[:, :]), "b_T")

            def c_turn(t, i):
                need(pe, "c_xn", t + 1)
                pe.wait_ge(c_in[i], tile_dmas(t, i))
                need(pe, "c_x3", t)
                turn(c0[:, 0:P], c_xn[:, :])
                sig(turn(c0[:, P:2 * P], cin1[i][:, :]), "c_T")

            def d_turn(t, i):
                need(pe, "d_q3", t + 1)
                need(pe, "d_GTs", t)
                sig(turn(d0[:, 0:P], d_q3[:, :], to_alternating), "d_T")

            def a_turn(t, i):
                need(pe, "a_xn", t + 1)
                pe.wait_ge(x_in[i], tile_dmas(t, i))
                need(pe, "a_x1", t)
                turn(bA[:, 0:P], a_xn[:, :])
                sig(turn(bA[:, P:2 * P], cin[i][:, :]), "a_T")

            def b_proj(t, i):
                need(pe, "b_XT", t + 1)
                need(pe, "b_OS1", t)
                need(pe, "z_x2", t - 1)
                sig(mm(b2[:, 0:2 * NG + XV], b_XT[:, :], m_wg[:, :]), "b_gx")
                for j in range(J0):
                    last = mm(b0[:, j * P:(j + 1) * P], m_wq[:, j * P:(j + 1) * P], b_XT[:, :])
                sig(last, "b_q")
                need(pe, "z_ZT", t - 1)
                need(pe, "b_P", t)
                for j in range(J0):
                    last = mm(b1[:, j * P:(j + 1) * P], m_wk[:, j * P:(j + 1) * P], b_XT[:, :])
                sig(last, "b_k")

            def c_proj(t, i):
                need(pe, "c_XT", t + 1)
                mm(c0[:, 0:P], c_wq[:, :], c_XT[:, 0, :])
                mm(c0[:, P:2 * P], c_wk[:, :], c_XT[:, 1, :])
                sig(mm(c0[:, 2 * P:3 * P], c_XT[:, 1, :], c_wv[:, :]), "c_qkv")

            def a_proj(t, i):
                need(pe, "a_XT", t + 1)
                mm(bA[:, 0:P], a_wq[:, :], a_XT[:, 0, :])
                mm(bA[:, P:2 * P], a_wk[:, :], a_XT[:, 1, :])
                sig(mm(bA[:, 2 * P:3 * P], a_XT[:, 1, :], a_wv[:, :]), "a_qkv")

            def d_hidden(t, i):
                need(pe, "d_XP", t + 1)
                need(pe, "d_out", t)
                mm(d1[:, :], onesb[0:3, :], CB[:, :], True, False)
                for k in range(TAPS):
                    last = mm(d1[:, :], d_XP[:, 2 * k:2 * k + TOK], W1K[:, k, :], False, k == TAPS - 1)
                sig(last, "d_y")

            def b_scores(t, i):
                for e in ("b_Q0", "b_Q1", "b_K"):
                    need(pe, e, t + 1)
                for j in range(J0):
                    for b in range(2):
                        last = mm(b0[:, (2 * j + b) * SEQ:(2 * j + b + 1) * SEQ],
                                  b_Q[:, j, b, :, :].rearrange("p h q -> p (h q)"),
                                  b_K[:, j, b * SEQ:(b + 1) * SEQ])
                sig(last, "b_S")

            def a_scores(t, i):
                for e in ("a_q", "a_k", "a_v"):
                    need(pe, e, t + 1)
                mm(bA[:, 0:P], a_Q[:, :], a_K[:, :], True, False)
                sig(mm(bA[:, 0:P], batch_b[:, 0, :], batch_b[:, 1, :], False, True), "a_S")

            def c_scores(t, i):
                for e in ("c_Q0", "c_Q1", "c_KM", "c_ng", "c_V1"):
                    need(pe, e, t + 1)
                for b, bk in ((0, c0), (1, c1)):
                    if b:
                        need(pe, "c_OTs", t)
                    o = bk[:, :].rearrange("p (j k) -> p j k", j=J1)
                    cols = slice(b * SEQ, (b + 1) * SEQ)
                    mm(o, c_Q[:, b, :, :].rearrange("p s q -> p (s q)"), c_KM[:, :, cols], True, False)
                    sig(mm(o, onesb[0:1, :], c_ng[:, cols].unsqueeze(1).broadcast_to([1, J1, SEQ]), False, True),
                        f"c_S{b}")

            def b_turnp(t, i):
                need(pe, "b_sub", t + 1)
                need(pe, "b_K", t + 1)
                for j in range(J0):
                    last = turn(b1[:, j * P:(j + 1) * P], b_D[:, j * P:(j + 1) * P])
                sig(last, "b_PT")

            def a_turnp(t, i):
                need(pe, "a_P", t + 1)
                sig(turn(bA[:, P:2 * P], a_P[:, :]), "a_PT")

            def a_mix(t, i):
                need(pe, "a_PTs", t + 1)
                sig(mm(bA[:, 2 * P:3 * P], a_PT[:, :], a_V[:, :]), "a_O")

            def c_turnp(t, i):
                need(pe, "c_sub0", t + 1)
                need(pe, "c_sub1", t + 1)
                for h, bk in ((0, c0), (1, c1)):
                    for j in range(4):
                        last = turn(bk[:, j * P:(j + 1) * P],
                                    c_D[:, 4 * h + j, :, :].rearrange("p b k -> p (b k)"))
                    sig(last, f"c_PT{h}")

            def d_turng(t, i):
                need(pe, "d_g2", t + 1)
                need(pe, "d_XP", t + 1)
                for c in range(HC):
                    last = turn(d0[:, c * P:(c + 1) * P], d_g2[:, c * P:(c + 1) * P], from_alternating)
                sig(last, "d_GT")

            def d_down(t, i):
                need(pe, "d_GTs", t + 1)
                need(pe, "d_g", t + 1)
                for c in range(HC):
                    last = mm(d1[:, 0:P], d_GT[:, c, :], W2T[:, c, :], c == 0, c == HC - 1)
                need(pe, "d_grs", t + 1)
                sig(mm(d1[:, P:P + 1], from_alternating[:, :], d_s[:, 12:13], True, True), "d_acc")

            def z_turn(t, i):
                need(pe, "z_Z", t + 1)
                need(pe, "b_P", t + 2 if not isinstance(t, int) else min(t + 2, TILES))
                for c in range(3):
                    last = turn(b1[:, c * P:(c + 1) * P], z_Z[:, c * P:(c + 1) * P])
                sig(last, "z_T")

            def z_down(t, i):
                need(pe, "z_ZT", t + 1)
                need(pe, "b_GX", t + 2 if not isinstance(t, int) else min(t + 2, TILES))
                for c in range(3):
                    last = mm(b2[:, 0:P], z_ZT[:, c * P:(c + 1) * P], m_wo[:, c, :], c == 0, c == 2)
                sig(last, "z_out")

            def c_values(t, i):
                need(pe, "c_P0", t + 1)
                need(pe, "c_P1", t + 1)
                for j in range(J1):
                    last = mm(c0[:, j * 36:(j + 1) * 36], c_PT[:, j * P:(j + 1) * P],
                              c_V[:, j, :, :, :].rearrange("p s b d -> p (s b d)"))
                sig(last, "c_O")

            def b_values(t, i):
                need(pe, "b_P", t + 1)
                need(pe, "b_V", t + 1)
                need(pe, "z_x2", t)
                gate(pe, "pe")
                for h in range(H0):
                    for b in range(2):
                        rows = slice(64 * b, 64 * b + 64)
                        at = (h % 4) * (DH + 1)
                        last = mm((b0, b2)[h // 4][rows, at:at + DH + 1], b_PT[rows, h * SEQ:(h + 1) * SEQ],
                                  b_V[rows, h, :])
                sig(last, "b_O")

            def c_turno(t, i):
                need(pe, "c_n0", t + 1)
                need(pe, "c_n1", t + 1)
                sig(turn(c1[:, 0:P], c_ON[:, :, :, :].rearrange("p b j d -> p (b j d)")), "c_OT")

            def c_down(t, i):
                need(pe, "c_OTs", t + 1)
                gate(pe, "pe")
                for b in range(2):
                    rows = slice(64 * b, 64 * b + 64)
                    for s in range(2):
                        last = mm(c0[rows, 0:P], c_OT[rows, s * SEQ:(s + 1) * SEQ], c_wo[rows, s, :], s == 0, s == 1)
                sig(last, "c_out")

            run(pe, [("moe", b_turn), ("attn1", c_turn), ("ffn", d_turn), ("attn0", a_turn),
                     ("moe", b_proj), ("attn1", c_proj), ("attn0", a_proj), ("ffn", d_hidden),
                     ("moe", b_scores), ("attn0", a_scores), ("attn1", c_scores),
                     ("moe", b_turnp), ("attn0", a_turnp), ("attn0", a_mix), ("attn1", c_turnp), ("ffn", d_turng), ("ffn", d_down),
                     ("mix", z_turn), ("mix", z_down), ("attn1", c_values), ("attn1", c_turno), ("attn1", c_down),
                     ("moe", b_values)])

        @block.vector
        def _(dve):
            dve.wait_ge(w_in, 16 * len(weights))
            dve.wait_ge(zeroed, 13)
            v = nc.vector
            done = [0]

            def st(ins, wait=False):
                done[0] += 1
                ins.then_inc(setup_v, 1)
                if wait:
                    dve.wait_ge(setup_v, done[0])

            st(v.tensor_scalar(c_bvw[:, :], ones[:, :], c_bv[:, :], None, ALU.mult))
            st(v.tensor_reduce(wstat[:, 0:1], w1raw[:, :, :].rearrange("p c d -> p (c d)"), AX, ALU.add,
                               apply_absolute_value=True))
            st(v.tensor_reduce(wstat[:, 1:2], w2raw[:, :], AX, ALU.add, apply_absolute_value=True))
            assert done[0] == SETUP_SUMS
            st(v.tensor_scalar(m_wg[:, 2 * NG:], m_wv[:, :], 0.5, None, ALU.mult))
            st(v.tensor_copy(batch_b[:, :, :], batch_f[:, :, :]))
            st(v.tensor_copy(cb_hi[:, :], convb[:, :]), True)
            st(v.tensor_tensor(cb_r1[:, :], convb[:, :], cb_hi[:, :], ALU.subtract), True)
            st(v.tensor_copy(cb_mid[:, :], cb_r1[:, :]), True)
            st(v.tensor_tensor(cb_r2[:, :], cb_r1[:, :], cb_mid[:, :], ALU.subtract), True)
            st(v.tensor_copy(cb_lo[:, :], cb_r2[:, :]), True)
            st(v.tensor_scalar(cb_s1[:, :], cb_hi[:, :], ident[0:3, 0:1], None, ALU.mult), True)
            st(v.scalar_tensor_tensor(cb_s2[:, :], cb_mid[:, :], ident[0:3, 1:2], cb_s1[:, :], ALU.mult, ALU.add), True)
            st(v.scalar_tensor_tensor(CB[:, :], cb_lo[:, :], ident[0:3, 2:3], cb_s2[:, :], ALU.mult, ALU.add))
            dve.wait_ge(setup_t, 2)
            st(v.tensor_tensor(c_bias[:, :], bA[:, 0:P], c_bo[:, :], ALU.add))
            st(v.tensor_scalar(wstat[:, 2:4], b0[:, 0:2], 1.0 / (HID * D), QCLIP, ALU.mult, ALU.max), True)
            st(v.reciprocal(wstat[:, 4:6], wstat[:, 2:4]), True)
            w1f, q1f = (a[:, :, :].rearrange("p c d -> p (c d)") for a in (w1raw, w1q))
            st(v.tensor_scalar(q1f, w1f, wstat[:, 4:5], ROUND, ALU.mult, ALU.add), True)
            st(v.tensor_scalar(q1f, q1f, ROUND, 1.0, ALU.subtract, ALU.min), True)
            st(v.tensor_scalar(q1f, q1f, -1.0, wstat[:, 2:3], ALU.max, ALU.mult), True)
            st(v.tensor_scalar(w2q[:, :], w2raw[:, :], wstat[:, 5:6], ROUND, ALU.mult, ALU.add), True)
            st(v.tensor_scalar(w2q[:, :], w2q[:, :], ROUND, 1.0, ALU.subtract, ALU.min), True)
            st(v.tensor_scalar(w2q[:, :], w2q[:, :], -1.0, None, ALU.max), True)
            assert done[0] == SETUP_Q
            for k in range(TAPS):
                for c in range(HC):
                    st(v.tensor_scalar(w1taps[:, k, c, :], w1q[:, c, :], convw[:, c, k:k + 1], None, ALU.mult))
            for k in range(TAPS):
                dve.wait_ge(setup_t, 3 + k)
                st(v.tensor_copy(W1K[:, k, :], (b1, b2, c0)[k][:, :]))
            dve.wait_ge(setup_t, 3 + TAPS)
            st(v.tensor_copy(W2T[:, :, :].rearrange("p c e -> p (c e)"), c1[:, :]))
            st(v.tensor_scalar(wstat[:, 6:7], wstat[:, 3:4], 0.5 / QMAX, None, ALU.mult), True)
            assert done[0] == SETUP_V

            def stats(s, tiles):
                def part(t, i):
                    if s == "x":
                        dve.wait_ge(x_in[i], tile_dmas(t, i))
                    else:
                        need(dve, {"x1": "a_x1", "x2": "z_x2", "x3": "c_x3"}[s], t + 1)
                    b = stat[s][i]
                    sig(v.bn_stats(b[:, 0:6], tiles[i][:, :]), s + "_bn")
                    need(dve, s + "_bn", t + 1)
                    gate(dve, "dve")
                    sig(v.bn_aggr(b[:, 6:8], b[:, 0:6]), s + "_stats")
                    need(dve, s + "_stats", t + 1)
                    sig(v.tensor_scalar(b[:, 8:9], b[:, 7:8], LN_EPS, None, ALU.add), s + "_var")
                return part

            def norm(s, tiles, o, done_, free):
                def part(t, i):
                    need(dve, s + "_rstd", t + 1)
                    need(dve, free, t)
                    b = stat[s][i]
                    sig(v.tensor_scalar(o[:, :], tiles[i][:, :], b[:, 6:7], b[:, 9:10], ALU.subtract, ALU.mult), done_)
                return part

            def c_masks(t, i):
                dve.wait_ge(c_in[i], tile_dmas(t, i))
                need(dve, "c_KM1", t)
                sig(v.tensor_copy(c_mf[:, :], mrow[i][:, :]), "c_mf")
                need(dve, "c_S1", t)
                sig(v.tensor_scalar(c_ng[:, :], mrow[i][0:1, :], MASK_BIG, -MASK_BIG, ALU.mult, ALU.add), "c_ng")

            def a_max(t, i):
                need(dve, "a_S", t + 1)
                sig(v.tensor_reduce(a_small[:, 0:1], bA[:, 0:P], AX, ALU.max, negate=True), "a_max")

            def a_end(t, i):
                need(dve, "a_P", t + 1)
                sig(v.reciprocal(a_small[:, 2:3], a_small[:, 1:2]), "a_recip")
                need(dve, "a_O", t + 1)
                need(dve, "a_recip", t + 1)
                need(dve, "a_xb", t + 1)
                need(dve, "z_x2", t - 1)
                sig(v.scalar_tensor_tensor(x1[i][:, :], bA[:, 2 * P:3 * P], a_small[:, 2:3], a_xb[:, :],
                                           ALU.mult, ALU.add), "a_x1")

            def b_gates(t, i):
                need(dve, "b_GX", t + 1)
                g = b_GX[:, 0:2 * NG].rearrange("p (h e) -> p h e", e=E)
                for d in range(1, E):
                    lower, upper = g[:, :, 0:E - d], g[:, :, d:E]
                    v.tensor_tensor(b_cmp[:, :, 0:E - d, d - 1], upper, lower, ALU.is_gt)
                    last = v.tensor_tensor(b_cmp[:, :, d:E, E - 1 - d], lower, upper, ALU.is_ge)
                sig(last, "b_cmp")
                need(dve, "b_cmp", t + 1)
                sig(v.tensor_reduce(b_rank[:, :], b_cmp[:, :, :, :].rearrange("p h e c -> p (h e) c"), AX, ALU.add), "b_rank")
                need(dve, "b_rank", t + 1)
                sig(v.tensor_scalar(b_mask[:, :], b_rank[:, :], 1.5, None, ALU.is_lt), "b_mask")
                need(dve, "b_mask", t + 1)
                need(dve, "b_th", t + 1)
                need(dve, "b_VP", t)
                sig(v.scalar_tensor_tensor(b_wv[:, :], b_th[:, :], 1.0, b_mask[:, 0:NG], ALU.add, ALU.mult), "b_wv")

            def b_softmax(t, i):
                need(dve, "b_S", t + 1)
                s = b0[:, :].rearrange("p (g k) -> p g k", g=8)
                sig(v.tensor_reduce(b_max[:, :], s, AX, ALU.max), "b_max")
                need(dve, "b_max", t + 1)
                need(dve, "b_PT", t)
                sig(v.tensor_tensor(b_D[:, :].rearrange("p (g k) -> p g k", g=8), s,
                                    b_max[:, :].unsqueeze(2).broadcast_to([P, 8, SEQ]), ALU.subtract), "b_sub")

            def c_softmax(t, i):
                for b, bk in ((0, c0), (1, c1)):
                    need(dve, f"c_S{b}", t + 1)
                    s = bk[:, :].rearrange("p (j k) -> p j k", j=J1)
                    sig(v.tensor_reduce(c_max[:, b, :], s, AX, ALU.max), f"c_max{b}")
                    need(dve, f"c_max{b}", t + 1)
                    need(dve, "c_PT1", t)
                    sig(v.tensor_tensor(c_D[:, :, b, :], s, c_max[:, b, :].unsqueeze(2).broadcast_to([P, J1, SEQ]),
                                        ALU.subtract), f"c_sub{b}")

            def z_sum(t, i):
                need(dve, "z_ZP", t + 1)
                sig(v.tensor_tensor(z_1[:, :, :], z_P[:, 0:4, :], z_P[:, 4:8, :], ALU.add), "z_1")
                need(dve, "z_1", t + 1)
                sig(v.tensor_tensor(z_2[:, :, :], z_1[:, 0:2, :], z_1[:, 2:4, :], ALU.add), "z_2")
                need(dve, "z_2", t + 1)
                need(dve, "z_T", t)
                sig(v.tensor_tensor(z_Z[:, 0:XV], z_2[:, 0, :], z_2[:, 1, :], ALU.add), "z_Z")

            def b_vsum(t, i):
                need(dve, "b_VP", t + 1)
                sig(v.tensor_tensor(b_V1[:, :, :], b_VP[:, 0:2, :], b_VP[:, 2:4, :], ALU.add), "b_v1")
                need(dve, "b_v1", t + 1)
                sig(v.tensor_tensor(b_V2[:, :], b_V1[:, 0, :], b_V1[:, 1, :], ALU.add), "b_v2")
                need(dve, "b_v2", t + 1)
                need(dve, "b_O", t)
                sig(v.tensor_tensor(b_V[:, :, 0:DH], b_V2[:, :].rearrange("p (h k) -> p h k", h=H0),
                                    b_VP[:, 4, :].rearrange("p (h k) -> p h k", h=H0), ALU.add), "b_V")

            def b_coef(t, i):
                need(dve, "b_OS0", t + 1)
                need(dve, "b_OS1", t + 1)
                sig(v.reciprocal(b_r[:, :].unsqueeze(2), b_O[:, :, DH:DH + 1]), "b_recip")
                need(dve, "b_recip", t + 1)
                need(dve, "z_ZP", t)
                sig(v.tensor_tensor(b_cf[:, :].rearrange("p (h e) -> p h e", e=E),
                                    b_mask[:, NG:2 * NG].rearrange("p (h e) -> p h e", e=E),
                                    b_r[:, :].unsqueeze(2).broadcast_to([P, H0, E]), ALU.mult), "b_cf")

            def z_end(t, i):
                need(dve, "z_out", t + 1)
                need(dve, "c_xn", t - 1)
                need(dve, "c_xb", t - 1)
                sig(v.tensor_tensor(x2[i][:, :], b2[:, 0:P], x1[i][:, :], ALU.add), "z_x2")

            def c_norm(t, i):
                need(dve, "c_O", t + 1)
                need(dve, "c_OT", t)
                for s in range(2):
                    rows = slice(64 * s, 64 * s + 64)
                    o = c0[rows, 0:36 * J1].rearrange("p (j s b d) -> p j s b d", j=J1, s=2, b=2)[:, :, s]
                    sig(v.reciprocal(c_r[rows, :, :].unsqueeze(3), o[:, :, :, HD:VW]), f"c_r{s}")
                for s in range(2):
                    rows = slice(64 * s, 64 * s + 64)
                    o = c0[rows, 0:36 * J1].rearrange("p (j s b d) -> p j s b d", j=J1, s=2, b=2)[:, :, s]
                    need(dve, f"c_r{s}", t + 1)
                    sig(v.tensor_tensor(c_ON[rows, :, :, :].rearrange("p b j d -> p j b d"), o[:, :, :, 0:HD],
                                        c_r[rows, :, :].unsqueeze(3).broadcast_to([64, J1, 2, HD]), ALU.mult), f"c_n{s}")

            def c_end(t, i):
                need(dve, "c_out", t + 1)
                need(dve, "c_xb", t + 1)
                need(dve, "d_out", t - 1)
                sig(v.tensor_tensor(x3[i][:, :], c0[:, 0:P], c_xb[:, :], ALU.add), "c_x3")

            def quant_scales(t, src, at, names, clip):
                am, cl, rc, sc = names
                sig(v.tensor_reduce(d_s[:, at:at + 1], src, AX, ALU.max, apply_absolute_value=True), am)
                need(dve, am, t + 1)
                sig(v.tensor_scalar(d_s[:, at + 1:at + 2], d_s[:, at:at + 1], clip, None, ALU.max), cl)
                need(dve, cl, t + 1)
                sig(v.reciprocal(d_s[:, at + 2:at + 3], d_s[:, at + 1:at + 2]), rc)
                need(dve, rc, t + 1)
                sig(v.tensor_scalar(d_s[:, at + 3:at + 4], d_s[:, at + 2:at + 3], QMAX, None, ALU.mult), sc)
                need(dve, sc, t + 1)

            def d_quant(t, i):
                need(dve, "d_xn", t + 1)
                quant_scales(t, d_xn[:, :], 0, ("d_am", "d_cl", "d_rc", "d_sc"), QCLIP)
                sig(v.tensor_scalar(d_s[:, 4:5], d_s[:, 1:2], 1.0 / QMAX, None, ALU.mult), "d_rs")
                sig(v.tensor_scalar(d_q1[:, :], d_xn[:, :], d_s[:, 3:4], QMAX, ALU.mult, ALU.min), "d_q1")
                need(dve, "d_q1", t + 1)
                sig(v.tensor_scalar(d_q2[:, :], d_q1[:, :], QMIN, ROUND, ALU.max, ALU.add), "d_q2")
                need(dve, "d_q2", t + 1)
                need(dve, "d_rs", t + 1)
                need(dve, "d_T", t)
                sig(v.tensor_scalar(d_q3[:, :], d_q2[:, :], ROUND, d_s[:, 4:5], ALU.subtract, ALU.mult), "d_q3")

            def d_act(t, i):
                need(dve, "d_th", t + 1)
                sig(v.scalar_tensor_tensor(d_g[:, :], d_th[:, :], 1.0, d1[:, :], ALU.add, ALU.mult), "d_g")
                need(dve, "d_g", t + 1)
                quant_scales(t, d_g[:, :], 8, ("d_gam", "d_gcl", "d_grc", "d_gsc"), 2 * QCLIP)
                sig(v.tensor_scalar(d_s[:, 12:13], d_s[:, 9:10], wstat[:, 6:7], None, ALU.mult), "d_grs")
                sig(v.tensor_scalar(d_g1[:, :], d_g[:, :], d_s[:, 11:12], QMAX, ALU.mult, ALU.min), "d_g1")
                need(dve, "d_g1", t + 1)
                need(dve, "d_GT", t)
                sig(v.tensor_scalar(d_g2[:, :], d_g1[:, :], QMIN, ROUND, ALU.max, ALU.add), "d_g2")

            def d_end(t, i):
                need(dve, "d_acc", t + 1)
                need(dve, "d_grs", t + 1)
                if not isinstance(t, int):
                    dve.wait_ge(y_out[i], (t - i) * 8)
                elif t > 1:
                    dve.wait_ge(y_out[i], 16 * (t // 2))
                sig(v.scalar_tensor_tensor(y[i][:, :], d1[:, 0:P], d1[:, P:P + 1], x3[i][:, :], ALU.mult, ALU.add), "d_out")

            run(dve, [("moe", norm("x1", x1, b_xn, "b_xn", "b_T")), ("attn1", norm("x2", x2, c_xn, "c_xn", "c_T")),
                      ("ffn", norm("x3", x3, d_xn, "d_xn", "d_q1")), ("attn0", norm("x", xin, a_xn, "a_xn", "a_T")),
                      ("ffn", d_quant), ("attn1", c_masks),
                      ("moe", b_gates), ("moe", b_softmax), ("attn0", a_max), ("attn1", c_softmax),
                      ("ffn", d_act), ("mix", z_sum), ("mix", z_end), ("attn0", a_end), ("attn1", c_norm), ("attn1", c_end),
                      ("ffn", d_end), ("moe", b_vsum), ("moe", b_coef),
                      ("stat", stats("x", xin)), ("mix", stats("x2", x2)), ("attn0", stats("x1", x1)),
                      ("attn1", stats("x3", x3))])


def kernel(**inputs):
    import numpy as np
    import concourse.bacc as bacc
    from concourse.bass_utils import run_bass_kernel_spmd as run_spmd

    nc = bacc.Bacc("TRN2", target_bir_lowering=False, num_devices=1)
    arrays = {}

    def give(name, a):
        a = np.ascontiguousarray(a)
        arrays[name] = a
        return nc.dram_tensor(name, a.shape, mybir.dt.from_np(a.dtype), kind="ExternalInput").ap()

    g = {n: np.asarray(a) for n, a in inputs.items()}
    column, row = (lambda a: a.reshape(-1, 1)), (lambda a: a.reshape(1, -1))
    w = {
        "a_wqT": g["L0_xattn_Wq"].T, "a_wkT": g["L0_xattn_Wk"].T, "a_wvT": g["L0_xattn_Wv"].T,
        "a_bq": column(g["L0_xattn_bq"]), "a_bk": column(g["L0_xattn_bk"]), "a_bv": row(g["L0_xattn_bv"]),
        "m_wq": g["L0_ffn_Wq"], "m_wk": g["L0_ffn_Wk"], "m_ws": g["L0_ffn_Ws"], "m_wd": g["L0_ffn_Wd"],
        "m_wv": g["L0_ffn_Wv"], "m_wo": g["L0_ffn_Wo"],
        "c_wqT": g["L1_xattn_Wq"].T, "c_wkT": g["L1_xattn_Wk"].T, "c_wvT": g["L1_xattn_Wv"].T,
        "c_bq": column(g["L1_xattn_bq"]), "c_bk": column(g["L1_xattn_bk"]), "c_bv": column(g["L1_xattn_bv"]),
        "c_woT": g["L1_xattn_Wo"].T, "c_bo": row(g["L1_xattn_bo"]),
        "w1": g["L1_ffn_w1"], "convw": g["L1_ffn_conv_w"], "convb": row(g["L1_ffn_conv_b"]), "w2": g["L1_ffn_w2"],
    }
    jmask = np.zeros((P, J1), np.float32)
    batch = np.zeros((2, 2, P), np.float32)
    alt = np.zeros((P, P), np.float32)
    for p in range(P):
        jmask[p, p // HD % J1] = 1.0
        batch[p // SEQ, 0, p] = 1.0
        alt[p, 2 * (p % SEQ) + p // SEQ] = 1.0
        batch[1 - p // SEQ, 1, p] = CROSS
    x = give("x_dram", g["x"])
    ctx1024 = give("ctx_dram", g["ctx_1024"])
    mask = give("mask_dram", g["mask_BxS2_bf1"])
    w = {n: give(n + "_dram", a) for n, a in w.items()}
    consts = {"ident": give("ident_dram", np.eye(P, dtype=np.float32)), "jmask": give("jmask_dram", jmask),
              "alt": give("alt_dram", alt), "altT": give("altT_dram", alt.T),
              "batch": give("batch_dram", batch)}
    out = nc.dram_tensor("out_dram", (NB, SEQ, D), F32, kind="ExternalOutput").ap()
    moe_transformer(nc, x, ctx1024, mask, w, consts, out)
    return run_spmd(nc, [arrays], core_ids=[0]).results[0]["out_dram"]
```

```python
from contextlib import ExitStack

import concourse.bass as bass
from concourse import mybir

F32 = mybir.dt.float32
BF16 = mybir.dt.bfloat16
U8 = mybir.dt.uint8
ALU = mybir.AluOpType
ACT = mybir.ActivationFunctionType
AX = mybir.AxisListType.X

P = 128
NB, SEQ, D = 128, 64, 128
TOK = P
TILES = NB * SEQ // TOK
LN_EPS = 1e-5
H0, DH, E = 8, 64, 5
J0 = H0 // 2
NG = H0 * E
XV = E * DH
ZW = 384
H1, HD = 16, 8
J1 = H1 // 2
VW = HD + 1
MASK_BIG = float(2 ** 27)
CROSS = -1e30
HID, TAPS = 512, 3
HC = HID // P
ROUND = float(1.5 * 2 ** 23)
QMAX, QCLIP = 127.0, 1e-5

LAG_MIN, LAG_MAX = -1, 5
LOOP_FROM, LOOP_TO = (LAG_MAX + 3) // 2 * 2, (TILES + LAG_MIN) // 2 * 2
SETUP_SUMS, SETUP_Q = 3, 23
SETUP_V = SETUP_Q + TAPS * HC + TAPS + 2

EVENTS = """x_stats x_rstd x1_stats x1_rstd x2_stats x2_rstd x3_stats x3_rstd
 a_xn a_T a_XT a_qkv a_q a_k a_v a_S a_max a_P a_recip a_PT a_PTs a_O a_x1 a_xb
 x_bn x1_bn x2_bn x3_bn x_var x1_var x2_var x3_var
 b_xn b_T b_XT b_gx b_q b_k b_GX b_Q0 b_Q1 b_K b_th b_cmp b_rank b_mask b_wv b_VP b_v1 b_v2 b_V
 b_S b_max b_E b_PT b_P b_O b_OS0 b_OS1 b_recip b_cf
 z_ZP z_1 z_2 z_Z z_T z_ZT z_out z_x2
 c_xn c_T c_XT c_qkv c_Q0 c_Q1 c_K c_V0 c_V1 c_mf c_KM1 c_KM c_ng c_S0 c_S1 c_max0 c_E0 c_max1 c_E1
 c_PT0 c_PT1 c_P0 c_P1 c_O c_r0 c_r1 c_n0 c_n1 c_OT c_OTs c_out c_x3 c_xb
 d_xn d_am d_cl d_rc d_sc d_rs d_q2 d_q3 d_T d_XP d_y d_th d_g d_gam d_gcl d_grc d_gsc d_grs d_g2
 d_GT d_GTs d_acc d_out""".split()


def moe_transformer(nc, x, ctx1024, mask, w, consts, out):
    x_rows = x.rearrange("b s d -> (b s) d")
    ctx_rows = ctx1024.rearrange("b s d -> (b s) d")
    out_rows = out.rearrange("b s d -> (b s) d")
    mask_row = mask.rearrange("(o b) s -> o (b s)", o=1)

    with ExitStack() as ctx:
        def sb(name, shape, dt=F32):
            return ctx.enter_context(nc.sbuf_tensor(name, shape, dt))

        def sem(name):
            return ctx.enter_context(nc.semaphore(name))

        bank = [ctx.enter_context(nc.psum_tensor(f"bank{i}", [P, 512], F32)) for i in range(8)]
        bA, b0, b1, b2, c0, c1, d0, d1 = bank

        ident = sb("ident", [P, P])
        to_alternating, from_alternating = sb("to_alternating", [P, P]), sb("from_alternating", [P, P])
        neground = sb("neground", [P, 1])
        ones = sb("ones", [P, P])
        halfneg = sb("halfneg", [P, 1])
        onesb = sb("onesb", [P, P], BF16)
        jmask = sb("jmask", [P, J1])
        batch_f = sb("batch_f", [2, 2, P])
        batch_b = sb("batch_b", [2, 2, P], BF16)
        a_wq, a_wk, a_wv = sb("a_wq", [P, P]), sb("a_wk", [P, P]), sb("a_wv", [P, P])
        a_bq, a_bk, a_bv = sb("a_bq", [P, 1]), sb("a_bk", [P, 1]), sb("a_bv", [P, P])
        m_wq, m_wk = sb("m_wq", [P, 512]), sb("m_wk", [P, 512])
        m_wg = sb("m_wg", [P, 2 * NG + XV])
        m_wv = sb("m_wv", [P, XV])
        m_wo = sb("m_wo", [P, 3, P])
        c_wq, c_wk, c_wv = sb("c_wq", [P, P]), sb("c_wk", [P, P]), sb("c_wv", [P, P])
        c_bq, c_bk = sb("c_bq", [P, 1]), sb("c_bk", [P, 1])
        c_wo = sb("c_wo", [P, 2, P])
        c_woT, c_bv, c_bo = sb("c_woT", [P, P]), sb("c_bv", [P, 1]), sb("c_bo", [P, P])
        c_bvw = sb("c_bvw", [P, P])
        c_bias = sb("c_bias", [P, P])
        w1raw, w2raw = sb("w1raw", [P, HC, P]), sb("w2raw", [P, HID])
        w1q, w2q = sb("w1q", [P, HC, P]), sb("w2q", [P, HID])
        wstat = sb("wstat", [P, 12])
        convw = sb("convw", [P, HC, TAPS])
        w1taps = sb("w1taps", [P, TAPS, HC, P])
        W1K = sb("W1K", [P, TAPS, HID])
        W2T = sb("W2T", [P, HC, P], BF16)
        convb = sb("convb", [3, HID])
        cb_hi, cb_mid, cb_lo = (sb(n, [3, HID], BF16) for n in ("cb_hi", "cb_mid", "cb_lo"))
        cb_r1, cb_r2, cb_s1, cb_s2 = (sb(n, [3, HID]) for n in ("cb_r1", "cb_r2", "cb_s1", "cb_s2"))
        CB = sb("CB", [3, HID], BF16)

        xin = [sb(f"xin{i}", [P, D]) for i in range(2)]
        cin = [sb(f"cin{i}", [P, D]) for i in range(2)]
        cin1 = [sb(f"cin1_{i}", [P, D]) for i in range(2)]
        mrow = [sb(f"mrow{i}", [P, TOK], U8) for i in range(2)]
        x1 = [sb(f"x1_{i}", [P, D]) for i in range(2)]
        x2 = [sb(f"x2_{i}", [P, D]) for i in range(2)]
        x3 = [sb(f"x3_{i}", [P, D]) for i in range(2)]
        y = [sb(f"y{i}", [P, D]) for i in range(2)]
        stat = {s: [sb(f"st_{s}{i}", [P, 16]) for i in range(2)] for s in ("x", "x1", "x2", "x3")}

        a_xn, a_XT = sb("a_xn", [P, P]), sb("a_XT", [P, 2, P])
        a_Q, a_K, a_V, a_P, a_PT = (sb(n, [P, P]) for n in ("a_Q", "a_K", "a_V", "a_P", "a_PT"))
        a_small, a_xb = sb("a_small", [P, 4]), sb("a_xb", [P, P])

        b_xn, b_XT = sb("b_xn", [P, P]), sb("b_XT", [P, P])
        b_GX = sb("b_GX", [P, 2 * NG + XV])
        b_Q = sb("b_Q", [P, J0, 2, 2, SEQ])
        b_K = sb("b_K", [P, J0, TOK])
        b_th, b_wv = sb("b_th", [P, NG]), sb("b_wv", [P, NG])
        b_cmp = sb("b_cmp", [P, 2 * H0, E, E - 1])
        b_rank, b_mask = sb("b_rank", [P, 2 * NG]), sb("b_mask", [P, 2 * NG])
        b_VP = sb("b_VP", [P, E, H0 * DH])
        b_V1, b_V2 = sb("b_V1", [P, 2, H0 * DH]), sb("b_V2", [P, H0 * DH])
        b_V = sb("b_V", [P, H0, DH + 1])
        b_max, b_E, b_PT = sb("b_max", [P, 8]), sb("b_E", [P, 512]), sb("b_PT", [P, 512])
        b_O = sb("b_O", [P, H0, DH + 1])
        b_r, b_cf = sb("b_r", [P, H0]), sb("b_cf", [P, NG])
        z_P = sb("z_P", [P, H0, XV])
        z_1, z_2 = sb("z_1", [P, 4, XV]), sb("z_2", [P, 2, XV])
        z_Z, z_ZT = sb("z_Z", [P, ZW]), sb("z_ZT", [P, ZW])

        c_xn, c_XT = sb("c_xn", [P, P]), sb("c_XT", [P, 2, P])
        c_Q = sb("c_Q", [P, 2, 2, SEQ])
        c_K, c_KM1 = sb("c_K", [P, P]), sb("c_KM1", [P, P])
        c_KM = sb("c_KM", [P, J1, TOK])
        c_mf = sb("c_mf", [P, TOK])
        c_ng = sb("c_ng", [1, TOK], BF16)
        c_V = sb("c_V", [P, J1, 2, 2, VW])
        c_max, c_E, c_PT = sb("c_max", [P, 2, J1]), sb("c_E", [P, J1, 2, SEQ]), sb("c_PT", [P, J1 * P])
        c_r, c_ON, c_OT = sb("c_r", [P, J1, 2]), sb("c_ON", [P, 2, J1, HD]), sb("c_OT", [P, P])
        c_xb = sb("c_xb", [P, P])

        d_xn, d_q2, d_q3 = (sb(n, [P, P]) for n in ("d_xn", "d_q2", "d_q3"))
        d_s = sb("d_s", [P, 16])
        d_XP = sb("d_XP", [P, (SEQ + 2) * 2])
        d_th, d_g, d_g2 = (sb(n, [P, HID]) for n in ("d_th", "d_g", "d_g2"))
        d_GT = sb("d_GT", [P, HC, P], BF16)

        ev = {n: sem(n) for n in EVENTS}
        x_in = [sem("x_in0"), sem("x_in1")]
        c_in = [sem("c_in0"), sem("c_in1")]
        y_out = [sem("y_out0"), sem("y_out1")]
        passed = {"pe": sem("pe_passed"), "dve": sem("dve_passed")}
        w_setup = sem("w_setup")
        w_in = sem("w_in")
        zeroed = sem("zeroed")
        setup_v, setup_t = sem("setup_v"), sem("setup_t")

        def need(eng, name, count):
            if not isinstance(count, int):
                eng.wait_ge(ev[name], count)
            elif count > 0:
                eng.wait_ge(ev[name], min(count, TILES))

        def gate(eng, name):
            eng.sem_inc(passed[name], 1)

        def sig(ins, name):
            return ins.then_inc(ev[name], 1)

        def tile_dmas(t, i):
            if isinstance(t, int):
                return 32 * (t // 2 + 1)
            return (t - i) * 16 + 32

        def step(program, n, par):
            for lag, part in program:
                t = n - lag
                if not isinstance(n, int) or 0 <= t < TILES:
                    part(t, (par + lag) % 2)

        def run(eng, program):
            assert all(LAG_MIN <= lag <= LAG_MAX for lag, _ in program)
            for n in range(LAG_MIN, LOOP_FROM):
                step(program, n, n % 2)
            with eng.Fori(LOOP_FROM // 2, LOOP_TO // 2) as i:
                for par in range(2):
                    step(program, 2 * i + par, par)
            for n in range(LOOP_TO, TILES + LAG_MAX):
                step(program, n, n % 2)

        setup_weights = [
            (w1raw[:, :, :], w["w1"].rearrange("(c p) d -> p c d", p=P)),
            (w2raw[:, :], w["w2"]), (c_bv[:, :], w["c_bv"]),
            (convb[:, :], w["convb"].broadcast_to([3, HID])), (ident[:, :], consts["ident"]),
            (c_woT[:, :], w["c_woT"]), (c_bo[:, :], w["c_bo"].broadcast_to([P, P])),
            (c_bq[:, :], w["c_bq"]), (batch_f[:, :, :], consts["batch"]),
            (convw[:, :, :], w["convw"].rearrange("(c p) o k -> p c (o k)", p=P)),
            (m_wv[:, :].rearrange("d (e k) -> d e k", e=E), w["m_wv"].rearrange("e d k -> d e k"))]
        weights = [
            (a_wq[:, :], w["a_wqT"]), (a_wk[:, :], w["a_wkT"]), (a_wv[:, :], w["a_wvT"]),
            (a_bq[:, :], w["a_bq"]), (a_bk[:, :], w["a_bk"]),
            (a_bv[:, :], w["a_bv"].broadcast_to([P, P])),
            (m_wq[:, :], w["m_wq"]), (m_wk[:, :], w["m_wk"]),
            (m_wg[:, 0:NG], w["m_ws"]), (m_wg[:, NG:2 * NG], w["m_wd"]),
            (m_wo[:, 0:2, :], w["m_wo"].rearrange("e k d -> (e k) d")[0:256, :].rearrange("(c p) d -> p c d", p=P)),
            (m_wo[0:DH, 2, :], w["m_wo"].rearrange("e k d -> (e k) d")[256:320, :]),
            (c_wq[:, :], w["c_wqT"]), (c_wk[:, :], w["c_wkT"]), (c_wv[:, :], w["c_wvT"]),
            (c_bk[:, :], w["c_bk"]), (jmask[:, :], consts["jmask"]),
            (c_wo[0:64, :, :], w["c_woT"].rearrange("(s r) e -> r s e", s=2)),
            (c_wo[64:128, :, :], w["c_woT"].rearrange("(s r) e -> r s e", s=2)),
            (to_alternating[:, :], consts["alt"]), (from_alternating[:, :], consts["altT"])]

        block = ctx.enter_context(nc.Block())

        @block.sync
        def _(sp):
            for dst, src in setup_weights:
                sp.dma_start(dst, src).then_inc(w_setup, 16)

            def load(t, i):
                need(sp, "a_xn", t - 1)
                need(sp, "a_xb", t - 1)
                need(sp, "x_bn", t - 1)
                need(sp, "a_T", t - 1)
                sp.dma_start(xin[i][:, :], x_rows[bass.ds(t * TOK, TOK), :]).then_inc(x_in[i], 16)
                sp.dma_start(cin[i][:, :], ctx_rows[bass.ds(t * TOK, TOK), :]).then_inc(x_in[i], 16)

            def load1(t, i):
                need(sp, "c_T", t - 1)
                need(sp, "c_ng", t - 1)
                sp.dma_start(cin1[i][:, :], ctx_rows[bass.ds(t * TOK, TOK), :]).then_inc(c_in[i], 16)
                sp.dma_start(mrow[i][:, :], mask_row[:, bass.ds(t * TOK, TOK)].broadcast_to([P, TOK])).then_inc(c_in[i], 16)

            def store(t, i):
                need(sp, "d_out", t + 1)
                sp.dma_start(out_rows[bass.ds(t * TOK, TOK), :], y[i][:, :]).then_inc(y_out[i], 16)

            run(sp, [(-1, load), (2, load1), (5, store)])
            for i in range(2):
                sp.wait_ge(y_out[i], 16 * (TILES // 2))

        @block.gpsimd
        def _(pool):
            fills = ((b_Q[:, :, :, :, :], 0.0), (c_Q[:, :, :, :], 0.0), (c_V[:, :, :, :, :], 0.0),
                     (z_Z[:, XV:ZW], 0.0), (m_wo[DH:P, 2, :], 0.0), (d_XP[:, :], 0.0),
                     (b_V[:, :, DH:DH + 1], 1.0), (ones[:, :], 1.0), (onesb[:, :], 1.0),
                     (neground[:, :], -ROUND), (halfneg[:, :], -0.5),
                     *((c_V[64 * b:64 * b + 64, :, :, b, HD:VW], 1.0) for b in range(2)))
            for n, (ap, value) in enumerate(fills):
                nc.gpsimd.memset(ap, value).then_inc(zeroed, 1)
                pool.wait_ge(zeroed, n + 1)
            pool.wait_ge(w_in, 16 * len(weights))
            pool.wait_ge(setup_v, SETUP_V)

            def rstd(s):
                def part(t, i):
                    need(pool, s + "_var", t + 1)
                    sig(nc.gpsimd.tensor_tensor(stat[s][i][:, 9:10], stat[s][i][:, 8:9], halfneg[:, :], ALU.pow),
                        s + "_rstd")
                return part

            def a_bias(t, i):
                pool.wait_ge(x_in[i], tile_dmas(t, i))
                need(pool, "a_x1", t)
                sig(nc.gpsimd.tensor_tensor(a_xb[:, :], xin[i][:, :], a_bv[:, :], ALU.add), "a_xb")

            def b_vprod(t, i):
                need(pool, "b_wv", t + 1)
                need(pool, "b_GX", t + 1)
                need(pool, "b_V", t)
                o = b_VP[:, :, :].rearrange("p e (h k) -> p e h k", h=H0)
                g = b_wv[:, :].rearrange("p (h e) -> p e h", e=E).unsqueeze(3).broadcast_to([P, E, H0, DH])
                v = b_GX[:, 2 * NG:].rearrange("p (e k) -> p e k", e=E).unsqueeze(2).broadcast_to([P, E, H0, DH])
                sig(nc.gpsimd.tensor_tensor(o, g, v, ALU.mult), "b_VP")

            def z_prod(t, i):
                need(pool, "b_cf", t + 1)
                need(pool, "b_OS0", t + 1)
                need(pool, "b_OS1", t + 1)
                need(pool, "z_1", t)
                o = z_P[:, :, :].rearrange("p h (e k) -> p h e k", e=E)
                a = b_O[:, :, 0:DH].unsqueeze(2).broadcast_to([P, H0, E, DH])
                c = b_cf[:, :].rearrange("p (h e) -> p h e", e=E).unsqueeze(3).broadcast_to([P, H0, E, DH])
                sig(nc.gpsimd.tensor_tensor(o, a, c, ALU.mult), "z_ZP")

            def b_vsum2(t, i):
                need(pool, "b_v1", t + 1)
                need(pool, "b_V", t)
                sig(nc.gpsimd.tensor_tensor(b_V2[:, :], b_V1[:, 0, :], b_V1[:, 1, :], ALU.add), "b_v2")

            def c_bias_add(t, i):
                need(pool, "z_x2", t + 1)
                need(pool, "c_x3", t)
                sig(nc.gpsimd.tensor_tensor(c_xb[:, :], x2[i][:, :], c_bias[:, :], ALU.add), "c_xb")

            def c_keys(t, i):
                need(pool, "c_K", t + 1)
                need(pool, "c_mf", t + 1)
                need(pool, "c_KM", t)
                sig(nc.gpsimd.tensor_tensor(c_KM1[:, :], c_K[:, :], c_mf[:, :], ALU.mult), "c_KM1")

            def c_spread(t, i):
                need(pool, "c_KM1", t + 1)
                need(pool, "c_S1", t)
                need(pool, "c_S0", t)
                sig(nc.gpsimd.tensor_tensor(c_KM[:, :, :], c_KM1[:, :].unsqueeze(1).broadcast_to([P, J1, TOK]),
                                            jmask[:, :].unsqueeze(2).broadcast_to([P, J1, TOK]), ALU.mult), "c_KM")

            rstd_x, rstd_x1, rstd_x2, rstd_x3 = (rstd(s) for s in stat)
            run(pool, [
                (0, rstd_x), (4, c_bias_add), (2, b_vsum2), (1, rstd_x1), (3, rstd_x2), (0, a_bias),
                (4, rstd_x3), (3, c_keys), (3, c_spread), (2, z_prod), (1, b_vprod)])

        @block.scalar
        def _(act):
            for dst, src in weights:
                act.dma_start(dst, src).then_inc(w_in, 16)
            act.wait_ge(setup_v, SETUP_V)
            act.wait_ge(zeroed, 13)
            act.wait_ge(w_in, 16 * len(weights))

            def copy(o, i_, name):
                return sig(nc.scalar.activation(o, i_, ACT.Copy), name)

            def c_masks(t, i):
                act.wait_ge(c_in[i], tile_dmas(t, i))
                need(act, "c_KM1", t)
                copy(c_mf[:, :], mrow[i][:, :], "c_mf")
                need(act, "c_S1", t)
                sig(nc.scalar.activation(c_ng[:, :], mrow[i][0:1, :], ACT.Copy, bias=-MASK_BIG, scale=MASK_BIG), "c_ng")

            def b_xt(t, i):
                need(act, "b_T", t + 1)
                need(act, "b_k", t)
                need(act, "b_gx", t)
                copy(b_XT[:, :], b0[:, 0:P], "b_XT")

            def c_xt(t, i):
                need(act, "c_T", t + 1)
                need(act, "c_qkv", t)
                copy(c_XT[:, :, :].rearrange("p a b -> p (a b)"), c0[:, 0:2 * P], "c_XT")

            def d_xt(t, i):
                need(act, "d_T", t + 1)
                need(act, "d_y", t)
                copy(d_XP[:, 2:2 + TOK], d0[:, 0:P], "d_XP")

            def a_xt(t, i):
                need(act, "a_T", t + 1)
                need(act, "a_qkv", t)
                copy(a_XT[:, :, :].rearrange("p a b -> p (a b)"), bA[:, 0:2 * P], "a_XT")

            def b_gxs(t, i):
                need(act, "b_gx", t + 1)
                need(act, "b_VP", t)
                need(act, "b_cmp", t)
                copy(b_GX[:, :], b2[:, 0:2 * NG + XV], "b_GX")

            def b_tanh(t, i):
                need(act, "b_GX", t + 1)
                need(act, "b_wv", t)
                sig(nc.scalar.activation(b_th[:, :], b_GX[:, 0:NG], ACT.Tanh, scale=0.5), "b_th")

            def b_qs(t, i):
                need(act, "b_q", t + 1)
                need(act, "b_S", t)
                for hh in range(2):
                    rows = slice(64 * hh, 64 * hh + 64)
                    sig(nc.scalar.activation(b_Q[rows, :, :, hh, :],
                                             b0[rows, :].rearrange("p (j b q) -> p j b q", j=J0, b=2),
                                             ACT.Copy, scale=float(DH) ** -0.5), f"b_Q{hh}")

            def b_ks(t, i):
                need(act, "b_S", t)
                need(act, "b_k", t + 1)
                copy(b_K[:, :, :].rearrange("p j s -> p (j s)"), b1[:, :], "b_K")

            def c_qs(t, i):
                need(act, "c_qkv", t + 1)
                need(act, "c_S1", t)
                for s in range(2):
                    rows = slice(64 * s, 64 * s + 64)
                    sig(nc.scalar.activation(c_Q[rows, :, s, :], c0[rows, 0:P].rearrange("p (b q) -> p b q", b=2),
                                             ACT.Identity, bias=c_bq[rows, :], scale=float(HD) ** -0.5), f"c_Q{s}")

            def c_ks(t, i):
                need(act, "c_qkv", t + 1)
                need(act, "c_KM1", t)
                sig(nc.scalar.activation(c_K[:, :], c0[:, P:2 * P], ACT.Identity, bias=c_bk[:, :]), "c_K")

            def c_vs(t, i):
                need(act, "c_qkv", t + 1)
                need(act, "c_O", t)
                for b in range(2):
                    rows = slice(64 * b, 64 * b + 64)
                    copy(c_V[rows, :, :, b, 0:HD].rearrange("p j s d -> p s j d"),
                         c0[rows, 2 * P:3 * P].rearrange("p (s j d) -> p s j d", s=2, j=J1), f"c_V{b}")

            def a_qkvs(t, i):
                need(act, "a_qkv", t + 1)
                need(act, "a_S", t)
                sig(nc.scalar.activation(a_Q[:, :], bA[:, 0:P], ACT.Identity, bias=a_bq[:, :]), "a_q")
                sig(nc.scalar.activation(a_K[:, :], bA[:, P:2 * P], ACT.Identity, bias=a_bk[:, :]), "a_k")
                need(act, "a_O", t)
                copy(a_V[:, :], bA[:, 2 * P:3 * P], "a_v")

            def d_tanh(t, i):
                need(act, "d_y", t + 1)
                need(act, "d_g", t)
                sig(nc.scalar.activation(d_th[:, :], d1[:, :], ACT.Tanh, scale=0.5), "d_th")

            def a_exp(t, i):
                need(act, "a_max", t + 1)
                need(act, "a_PT", t)
                need(act, "a_recip", t)
                sig(nc.scalar.activation(a_P[:, :], bA[:, 0:P], ACT.Exp, bias=a_small[:, 0:1],
                                         accum_out=a_small[:, 1:2]), "a_P")

            def b_exp(t, i):
                need(act, "b_max", t + 1)
                need(act, "b_PT", t)
                for g in range(8):
                    last = nc.scalar.activation(b_E[:, g * SEQ:(g + 1) * SEQ], b0[:, g * SEQ:(g + 1) * SEQ], ACT.Exp,
                                                bias=b_max[:, g:g + 1])
                sig(last, "b_E")

            def b_pt(t, i):
                need(act, "b_PT", t + 1)
                need(act, "b_O", t)
                copy(b_PT[:, :], b1[:, :], "b_P")

            def a_pt(t, i):
                need(act, "a_PT", t + 1)
                need(act, "a_O", t)
                copy(a_PT[:, :], bA[:, P:2 * P], "a_PTs")

            def c_exps(b, bk):
                def part(t, i):
                    need(act, f"c_max{b}", t + 1)
                    need(act, "c_PT1", t)
                    need(act, "c_PT0", t)
                    for j in range(J1):
                        last = nc.scalar.activation(c_E[:, j, b, :], bk[:, j * SEQ:(j + 1) * SEQ], ACT.Exp,
                                                    bias=c_max[:, b, j:j + 1])
                    sig(last, f"c_E{b}")
                return part

            def c_pt(h, bk):
                def part(t, i):
                    need(act, f"c_PT{h}", t + 1)
                    need(act, "c_O", t)
                    copy(c_PT[:, h * 512:(h + 1) * 512], bk[:, :], f"c_P{h}")
                return part

            def d_gt(t, i):
                need(act, "d_GT", t + 1)
                need(act, "d_acc", t)
                sig(nc.scalar.activation(d_GT[:, :, :].rearrange("p c s -> p (c s)"), d0[:, :], ACT.Identity,
                                         bias=neground[:, :]), "d_GTs")

            def z_t(t, i):
                need(act, "z_T", t + 1)
                need(act, "z_out", t)
                copy(z_ZT[:, :], b1[:, 0:ZW], "z_ZT")

            def b_os(t, i):
                need(act, "b_O", t + 1)
                need(act, "z_ZP", t)
                need(act, "b_recip", t)
                copy(b_O[:, 0:4, :].rearrange("p h k -> p (h k)"), b0[:, 0:4 * (DH + 1)], "b_OS0")
                copy(b_O[:, 4:8, :].rearrange("p h k -> p (h k)"), b2[:, 0:4 * (DH + 1)], "b_OS1")

            def c_ot(t, i):
                need(act, "c_OT", t + 1)
                need(act, "c_out", t)
                copy(c_OT[:, :], c1[:, 0:P], "c_OTs")

            c_exps0, c_exps1, c_pt0, c_pt1 = c_exps(0, c0), c_exps(1, c1), c_pt(0, c0), c_pt(1, c1)
            run(act, [
                (1, a_exp), (4, c_exps0), (5, d_xt), (2, b_exp), (3, c_masks), (4, c_exps1), (2, b_pt),
                (1, a_pt), (4, c_pt0), (3, z_t), (4, c_pt1), (0, a_xt), (5, d_tanh), (4, c_ot), (2, b_os),
                (0, a_qkvs), (3, c_xt), (1, b_xt), (3, c_ks), (3, c_vs), (3, c_qs), (1, b_gxs), (1, b_tanh),
                (5, d_gt), (1, b_ks), (1, b_qs)])

        @block.tensor
        def _(pe):
            pe.wait_ge(w_setup, 16 * len(setup_weights))
            pe.wait_ge(zeroed, 13)
            pe.wait_ge(setup_v, SETUP_SUMS)
            nc.tensor.matmul(bA[:, 0:P], c_bvw[:, :], c_woT[:, :], start=True, stop=True).then_inc(setup_t, 1)
            nc.tensor.matmul(b0[:, 0:2], ones[:, :], wstat[:, 0:2], start=True, stop=True).then_inc(setup_t, 1)
            for k in range(TAPS):
                pe.wait_ge(setup_v, SETUP_Q + HC * (k + 1))
                for c in range(HC):
                    last = nc.tensor.transpose([b1, b2, c0][k][:, c * P:(c + 1) * P], w1taps[:, k, c, :], ident[:, :])
                last.then_inc(setup_t, 1)
            for c in range(HC):
                last = nc.tensor.transpose(c1[:, c * P:(c + 1) * P], w2q[:, c * P:(c + 1) * P], ident[:, :])
            last.then_inc(setup_t, 1)
            pe.wait_ge(w_in, 16 * len(weights))
            pe.wait_ge(setup_v, SETUP_V)

            def mm(o, l, r, start=True, stop=True):
                return nc.tensor.matmul(o, l, r, start=start, stop=stop)

            def turn(o, a, order=ident):
                return nc.tensor.transpose(o, a, order[:, :])

            def b_turn(t, i):
                need(pe, "b_xn", t + 1)
                need(pe, "b_OS0", t)
                sig(turn(b0[:, 0:P], b_xn[:, :]), "b_T")

            def c_turn(t, i):
                need(pe, "c_xn", t + 1)
                pe.wait_ge(c_in[i], tile_dmas(t, i))
                need(pe, "c_x3", t)
                turn(c0[:, 0:P], c_xn[:, :])
                sig(turn(c0[:, P:2 * P], cin1[i][:, :]), "c_T")

            def d_turn(t, i):
                need(pe, "d_q3", t + 1)
                need(pe, "d_GTs", t)
                sig(turn(d0[:, 0:P], d_q3[:, :], to_alternating), "d_T")

            def a_turn(t, i):
                need(pe, "a_xn", t + 1)
                pe.wait_ge(x_in[i], tile_dmas(t, i))
                need(pe, "a_x1", t)
                turn(bA[:, 0:P], a_xn[:, :])
                sig(turn(bA[:, P:2 * P], cin[i][:, :]), "a_T")

            def b_gatevals(t, i):
                need(pe, "b_XT", t + 1)
                need(pe, "b_OS1", t)
                need(pe, "z_x2", t - 1)
                sig(mm(b2[:, 0:2 * NG + XV], b_XT[:, :], m_wg[:, :]), "b_gx")

            def b_queries(t, i):
                need(pe, "b_XT", t + 1)
                for j in range(J0):
                    last = mm(b0[:, j * P:(j + 1) * P], m_wq[:, j * P:(j + 1) * P], b_XT[:, :])
                sig(last, "b_q")

            def b_keys(t, i):
                need(pe, "b_XT", t + 1)
                need(pe, "z_ZT", t - 1)
                need(pe, "b_P", t)
                for j in range(J0):
                    last = mm(b1[:, j * P:(j + 1) * P], m_wk[:, j * P:(j + 1) * P], b_XT[:, :])
                sig(last, "b_k")

            def c_proj(t, i):
                need(pe, "c_XT", t + 1)
                mm(c0[:, 0:P], c_wq[:, :], c_XT[:, 0, :])
                mm(c0[:, P:2 * P], c_wk[:, :], c_XT[:, 1, :])
                sig(mm(c0[:, 2 * P:3 * P], c_XT[:, 1, :], c_wv[:, :]), "c_qkv")

            def a_proj(t, i):
                need(pe, "a_XT", t + 1)
                mm(bA[:, 0:P], a_wq[:, :], a_XT[:, 0, :])
                mm(bA[:, P:2 * P], a_wk[:, :], a_XT[:, 1, :])
                sig(mm(bA[:, 2 * P:3 * P], a_XT[:, 1, :], a_wv[:, :]), "a_qkv")

            def d_hidden(t, i):
                need(pe, "d_XP", t + 1)
                need(pe, "d_out", t)
                mm(d1[:, :], onesb[0:3, :], CB[:, :], True, False)
                for k in range(TAPS):
                    last = mm(d1[:, :], d_XP[:, 2 * k:2 * k + TOK], W1K[:, k, :], False, k == TAPS - 1)
                sig(last, "d_y")

            def b_scores(t, i):
                for e in ("b_Q0", "b_Q1", "b_K"):
                    need(pe, e, t + 1)
                for j in range(J0):
                    for b in range(2):
                        last = mm(b0[:, (2 * j + b) * SEQ:(2 * j + b + 1) * SEQ],
                                  b_Q[:, j, b, :, :].rearrange("p h q -> p (h q)"),
                                  b_K[:, j, b * SEQ:(b + 1) * SEQ])
                sig(last, "b_S")

            def a_scores(t, i):
                for e in ("a_q", "a_k", "a_v"):
                    need(pe, e, t + 1)
                mm(bA[:, 0:P], a_Q[:, :], a_K[:, :], True, False)
                sig(mm(bA[:, 0:P], batch_b[:, 0, :], batch_b[:, 1, :], False, True), "a_S")

            def c_scores(b, bk):
                def part(t, i):
                    for e in ("c_Q0", "c_Q1", "c_K", "c_KM", "c_ng", "c_V1"):
                        need(pe, e, t + 1)
                    if b:
                        need(pe, "c_OTs", t)
                    o = bk[:, :].rearrange("p (j k) -> p j k", j=J1)
                    cols = slice(b * SEQ, (b + 1) * SEQ)
                    mm(o, c_Q[:, b, :, :].rearrange("p s q -> p (s q)"), c_KM[:, :, cols], True, False)
                    sig(mm(o, onesb[0:1, :], c_ng[:, cols].unsqueeze(1).broadcast_to([1, J1, SEQ]), False, True),
                        f"c_S{b}")
                return part

            def b_turnp(t, i):
                need(pe, "b_E", t + 1)
                need(pe, "b_K", t + 1)
                for j in range(J0):
                    last = turn(b1[:, j * P:(j + 1) * P], b_E[:, j * P:(j + 1) * P])
                sig(last, "b_PT")

            def a_turnp(t, i):
                need(pe, "a_P", t + 1)
                sig(turn(bA[:, P:2 * P], a_P[:, :]), "a_PT")

            def a_mix(t, i):
                need(pe, "a_PTs", t + 1)
                sig(mm(bA[:, 2 * P:3 * P], a_PT[:, :], a_V[:, :]), "a_O")

            def c_turnp(h, bk):
                def part(t, i):
                    need(pe, "c_E0", t + 1)
                    need(pe, "c_E1", t + 1)
                    for j in range(4):
                        last = turn(bk[:, j * P:(j + 1) * P],
                                    c_E[:, 4 * h + j, :, :].rearrange("p b k -> p (b k)"))
                    sig(last, f"c_PT{h}")
                return part

            def d_turng(t, i):
                need(pe, "d_g2", t + 1)
                need(pe, "d_XP", t + 1)
                for c in range(HC):
                    last = turn(d0[:, c * P:(c + 1) * P], d_g2[:, c * P:(c + 1) * P], from_alternating)
                sig(last, "d_GT")

            def d_down(t, i):
                need(pe, "d_GTs", t + 1)
                need(pe, "d_g", t + 1)
                for c in range(HC):
                    last = mm(d1[:, 0:P], d_GT[:, c, :], W2T[:, c, :], c == 0, c == HC - 1)
                need(pe, "d_grs", t + 1)
                sig(mm(d1[:, P:P + 1], from_alternating[:, :], d_s[:, 12:13], True, True), "d_acc")

            def z_turn(t, i):
                need(pe, "z_Z", t + 1)
                need(pe, "b_P", t + 2)
                for c in range(3):
                    last = turn(b1[:, c * P:(c + 1) * P], z_Z[:, c * P:(c + 1) * P])
                sig(last, "z_T")

            def z_down(t, i):
                need(pe, "z_ZT", t + 1)
                need(pe, "b_GX", t + 2)
                for c in range(3):
                    last = mm(b2[:, 0:P], z_ZT[:, c * P:(c + 1) * P], m_wo[:, c, :], c == 0, c == 2)
                sig(last, "z_out")

            def c_values(t, i):
                need(pe, "c_P0", t + 1)
                need(pe, "c_P1", t + 1)
                for j in range(J1):
                    last = mm(c0[:, j * 36:(j + 1) * 36], c_PT[:, j * P:(j + 1) * P],
                              c_V[:, j, :, :, :].rearrange("p s b d -> p (s b d)"))
                sig(last, "c_O")

            def b_values(t, i):
                need(pe, "b_P", t + 1)
                need(pe, "b_V", t + 1)
                need(pe, "z_x2", t)
                gate(pe, "pe")
                for h in range(H0):
                    for b in range(2):
                        rows = slice(64 * b, 64 * b + 64)
                        at = (h % 4) * (DH + 1)
                        last = mm((b0, b2)[h // 4][rows, at:at + DH + 1], b_PT[rows, h * SEQ:(h + 1) * SEQ],
                                  b_V[rows, h, :])
                sig(last, "b_O")

            def c_turno(t, i):
                need(pe, "c_n0", t + 1)
                need(pe, "c_n1", t + 1)
                sig(turn(c1[:, 0:P], c_ON[:, :, :, :].rearrange("p b j d -> p (b j d)")), "c_OT")

            def c_down(t, i):
                need(pe, "c_OTs", t + 1)
                gate(pe, "pe")
                for b in range(2):
                    rows = slice(64 * b, 64 * b + 64)
                    for s in range(2):
                        last = mm(c0[rows, 0:P], c_OT[rows, s * SEQ:(s + 1) * SEQ], c_wo[rows, s, :], s == 0, s == 1)
                sig(last, "c_out")

            c_scores0, c_scores1, c_turnp0, c_turnp1 = c_scores(0, c0), c_scores(1, c1), c_turnp(0, c0), c_turnp(1, c1)
            run(pe, [
                (2, b_scores), (5, d_turn), (4, c_scores1), (5, d_hidden), (2, b_turnp), (1, a_turnp),
                (4, c_turnp0), (3, z_turn), (4, c_turnp1), (1, a_mix), (3, z_down), (4, c_values), (0, a_turn),
                (2, b_values), (4, c_turno), (0, a_proj), (4, c_down), (3, c_turn), (0, a_scores), (1, b_turn),
                (3, c_proj), (1, b_gatevals), (5, d_turng), (1, b_keys), (1, b_queries), (5, d_down),
                (3, c_scores0)])

        @block.vector
        def _(dve):
            dve.wait_ge(w_setup, 16 * len(setup_weights))
            dve.wait_ge(zeroed, 13)
            v = nc.vector
            done = [0]

            def st(ins, wait=False):
                done[0] += 1
                ins.then_inc(setup_v, 1)
                if wait:
                    dve.wait_ge(setup_v, done[0])

            st(v.tensor_scalar(c_bvw[:, :], ones[:, :], c_bv[:, :], None, ALU.mult))
            st(v.tensor_reduce(wstat[:, 0:1], w1raw[:, :, :].rearrange("p c d -> p (c d)"), AX, ALU.add,
                               apply_absolute_value=True))
            st(v.tensor_reduce(wstat[:, 1:2], w2raw[:, :], AX, ALU.add, apply_absolute_value=True))
            assert done[0] == SETUP_SUMS
            st(v.tensor_scalar(c_bq[:, :], c_bq[:, :], float(HD) ** -0.5, None, ALU.mult))
            st(v.tensor_scalar(m_wg[:, 2 * NG:], m_wv[:, :], 0.5, None, ALU.mult))
            st(v.tensor_copy(batch_b[:, :, :], batch_f[:, :, :]))
            st(v.tensor_copy(cb_hi[:, :], convb[:, :]), True)
            st(v.tensor_tensor(cb_r1[:, :], convb[:, :], cb_hi[:, :], ALU.subtract), True)
            st(v.tensor_copy(cb_mid[:, :], cb_r1[:, :]), True)
            st(v.tensor_tensor(cb_r2[:, :], cb_r1[:, :], cb_mid[:, :], ALU.subtract), True)
            st(v.tensor_copy(cb_lo[:, :], cb_r2[:, :]), True)
            st(v.tensor_scalar(cb_s1[:, :], cb_hi[:, :], ident[0:3, 0:1], None, ALU.mult), True)
            st(v.scalar_tensor_tensor(cb_s2[:, :], cb_mid[:, :], ident[0:3, 1:2], cb_s1[:, :], ALU.mult, ALU.add), True)
            st(v.scalar_tensor_tensor(CB[:, :], cb_lo[:, :], ident[0:3, 2:3], cb_s2[:, :], ALU.mult, ALU.add))
            dve.wait_ge(setup_t, 2)
            st(v.tensor_tensor(c_bias[:, :], bA[:, 0:P], c_bo[:, :], ALU.add))
            st(v.tensor_scalar(wstat[:, 2:4], b0[:, 0:2], 1.0 / (HID * D), QCLIP, ALU.mult, ALU.max), True)
            st(v.reciprocal(wstat[:, 4:6], wstat[:, 2:4]), True)
            w1f, q1f = (a[:, :, :].rearrange("p c d -> p (c d)") for a in (w1raw, w1q))
            st(v.tensor_scalar(q1f, w1f, wstat[:, 4:5], ROUND, ALU.mult, ALU.add), True)
            st(v.tensor_scalar(q1f, q1f, ROUND, 1.0, ALU.subtract, ALU.min), True)
            st(v.tensor_scalar(q1f, q1f, -1.0, wstat[:, 2:3], ALU.max, ALU.mult), True)
            st(v.tensor_scalar(w2q[:, :], w2raw[:, :], wstat[:, 5:6], ROUND, ALU.mult, ALU.add), True)
            st(v.tensor_scalar(w2q[:, :], w2q[:, :], ROUND, 1.0, ALU.subtract, ALU.min), True)
            st(v.tensor_scalar(w2q[:, :], w2q[:, :], -1.0, None, ALU.max), True)
            assert done[0] == SETUP_Q
            for k in range(TAPS):
                for c in range(HC):
                    st(v.tensor_scalar(w1taps[:, k, c, :], w1q[:, c, :], convw[:, c, k:k + 1], None, ALU.mult))
            for k in range(TAPS):
                dve.wait_ge(setup_t, 3 + k)
                st(v.tensor_copy(W1K[:, k, :], (b1, b2, c0)[k][:, :]))
            dve.wait_ge(setup_t, 3 + TAPS)
            st(v.tensor_copy(W2T[:, :, :].rearrange("p c e -> p (c e)"), c1[:, :]))
            st(v.tensor_scalar(wstat[:, 6:7], wstat[:, 3:4], 0.5 / QMAX, None, ALU.mult), True)
            assert done[0] == SETUP_V

            def bn(s, tiles):
                def part(t, i):
                    if s == "x":
                        dve.wait_ge(x_in[i], tile_dmas(t, i))
                    else:
                        need(dve, {"x1": "a_x1", "x2": "z_x2", "x3": "c_x3"}[s], t + 1)
                    sig(v.bn_stats(stat[s][i][:, 0:6], tiles[i][:, :]), s + "_bn")
                return part

            def aggr(s):
                def part(t, i):
                    need(dve, s + "_bn", t + 1)
                    gate(dve, "dve")
                    sig(v.bn_aggr(stat[s][i][:, 6:8], stat[s][i][:, 0:6]), s + "_stats")
                return part

            def vareps(s):
                def part(t, i):
                    need(dve, s + "_stats", t + 1)
                    sig(v.tensor_scalar(stat[s][i][:, 8:9], stat[s][i][:, 7:8], LN_EPS, None, ALU.add), s + "_var")
                return part

            def norm(s, tiles, o, done_, free):
                def part(t, i):
                    need(dve, s + "_rstd", t + 1)
                    for f in free:
                        need(dve, f, t)
                    b = stat[s][i]
                    sig(v.tensor_scalar(o[:, :], tiles[i][:, :], b[:, 6:7], b[:, 9:10], ALU.subtract, ALU.mult), done_)
                return part

            def a_max(t, i):
                need(dve, "a_S", t + 1)
                sig(v.tensor_reduce(a_small[:, 0:1], bA[:, 0:P], AX, ALU.max, negate=True), "a_max")

            def a_recip(t, i):
                need(dve, "a_P", t + 1)
                sig(v.reciprocal(a_small[:, 2:3], a_small[:, 1:2]), "a_recip")

            def a_end(t, i):
                need(dve, "a_O", t + 1)
                need(dve, "a_recip", t + 1)
                need(dve, "a_xb", t + 1)
                need(dve, "z_x2", t - 1)
                sig(v.scalar_tensor_tensor(x1[i][:, :], bA[:, 2 * P:3 * P], a_small[:, 2:3], a_xb[:, :],
                                           ALU.mult, ALU.add), "a_x1")

            def b_compare(t, i):
                need(dve, "b_GX", t + 1)
                g = b_GX[:, 0:2 * NG].rearrange("p (h e) -> p h e", e=E)
                for d in range(1, E):
                    lower, upper = g[:, :, 0:E - d], g[:, :, d:E]
                    v.tensor_tensor(b_cmp[:, :, 0:E - d, d - 1], upper, lower, ALU.is_gt)
                    last = v.tensor_tensor(b_cmp[:, :, d:E, E - 1 - d], lower, upper, ALU.is_ge)
                sig(last, "b_cmp")

            def b_ranks(t, i):
                need(dve, "b_cmp", t + 1)
                sig(v.tensor_reduce(b_rank[:, :], b_cmp[:, :, :, :].rearrange("p h e c -> p (h e) c"), AX, ALU.add), "b_rank")

            def b_masks(t, i):
                need(dve, "b_rank", t + 1)
                sig(v.tensor_scalar(b_mask[:, :], b_rank[:, :], 1.5, None, ALU.is_lt), "b_mask")

            def b_vgates(t, i):
                need(dve, "b_mask", t + 1)
                need(dve, "b_th", t + 1)
                need(dve, "b_VP", t)
                sig(v.scalar_tensor_tensor(b_wv[:, :], b_th[:, :], 1.0, b_mask[:, 0:NG], ALU.add, ALU.mult), "b_wv")

            b_groups = b0[:, :].rearrange("p (g k) -> p g k", g=8)

            def b_maxes(t, i):
                need(dve, "b_S", t + 1)
                sig(v.tensor_reduce(b_max[:, :], b_groups, AX, ALU.max, negate=True), "b_max")

            def c_maxes(b, bk):
                def part(t, i):
                    need(dve, f"c_S{b}", t + 1)
                    sig(v.tensor_reduce(c_max[:, b, :], bk[:, :].rearrange("p (j k) -> p j k", j=J1), AX, ALU.max,
                                        negate=True), f"c_max{b}")
                return part

            def z_sum1(t, i):
                need(dve, "z_ZP", t + 1)
                sig(v.tensor_tensor(z_1[:, :, :], z_P[:, 0:4, :], z_P[:, 4:8, :], ALU.add), "z_1")

            def z_sum2(t, i):
                need(dve, "z_1", t + 1)
                sig(v.tensor_tensor(z_2[:, :, :], z_1[:, 0:2, :], z_1[:, 2:4, :], ALU.add), "z_2")

            def z_sum3(t, i):
                need(dve, "z_2", t + 1)
                need(dve, "z_T", t)
                sig(v.tensor_tensor(z_Z[:, 0:XV], z_2[:, 0, :], z_2[:, 1, :], ALU.add), "z_Z")

            def b_vsum1(t, i):
                need(dve, "b_VP", t + 1)
                need(dve, "b_v2", t)
                sig(v.tensor_tensor(b_V1[:, :, :], b_VP[:, 0:2, :], b_VP[:, 2:4, :], ALU.add), "b_v1")

            def b_vsum3(t, i):
                need(dve, "b_v2", t + 1)
                need(dve, "b_O", t)
                sig(v.tensor_tensor(b_V[:, :, 0:DH], b_V2[:, :].rearrange("p (h k) -> p h k", h=H0),
                                    b_VP[:, 4, :].rearrange("p (h k) -> p h k", h=H0), ALU.add), "b_V")

            def b_recips(t, i):
                need(dve, "b_OS0", t + 1)
                need(dve, "b_OS1", t + 1)
                sig(v.reciprocal(b_r[:, :].unsqueeze(2), b_O[:, :, DH:DH + 1]), "b_recip")

            def b_coef(t, i):
                need(dve, "b_recip", t + 1)
                need(dve, "z_ZP", t)
                sig(v.tensor_tensor(b_cf[:, :].rearrange("p (h e) -> p h e", e=E),
                                    b_mask[:, NG:2 * NG].rearrange("p (h e) -> p h e", e=E),
                                    b_r[:, :].unsqueeze(2).broadcast_to([P, H0, E]), ALU.mult), "b_cf")

            def z_end(t, i):
                need(dve, "z_out", t + 1)
                need(dve, "c_xn", t - 1)
                need(dve, "c_xb", t - 1)
                sig(v.tensor_tensor(x2[i][:, :], b2[:, 0:P], x1[i][:, :], ALU.add), "z_x2")

            def c_out_of(s):
                return c0[64 * s:64 * s + 64, 0:36 * J1].rearrange("p (j s b d) -> p j s b d", j=J1, s=2, b=2)[:, :, s]

            def c_recips(t, i):
                need(dve, "c_O", t + 1)
                for s in range(2):
                    sig(v.reciprocal(c_r[64 * s:64 * s + 64, :, :].unsqueeze(3), c_out_of(s)[:, :, :, HD:VW]), f"c_r{s}")

            def c_normalise(t, i):
                need(dve, "c_OT", t)
                for s in range(2):
                    rows = slice(64 * s, 64 * s + 64)
                    need(dve, f"c_r{s}", t + 1)
                    sig(v.tensor_tensor(c_ON[rows, :, :, :].rearrange("p b j d -> p j b d"), c_out_of(s)[:, :, :, 0:HD],
                                        c_r[rows, :, :].unsqueeze(3).broadcast_to([64, J1, 2, HD]), ALU.mult), f"c_n{s}")

            def c_end(t, i):
                need(dve, "c_out", t + 1)
                need(dve, "c_xb", t + 1)
                need(dve, "d_out", t - 1)
                sig(v.tensor_tensor(x3[i][:, :], c0[:, 0:P], c_xb[:, :], ALU.add), "c_x3")

            def absmax(src, at, after, name):
                def part(t, i):
                    need(dve, after, t + 1)
                    sig(v.tensor_reduce(d_s[:, at:at + 1], src[:, :], AX, ALU.max, apply_absolute_value=True), name)
                return part

            def one(at, op, operand, of, after, name, free=None):
                def part(t, i):
                    need(dve, after, t + 1)
                    if free:
                        need(dve, free, t)
                    o, a = d_s[:, at:at + 1], d_s[:, of:of + 1]
                    sig(v.reciprocal(o, a) if op is None else v.tensor_scalar(o, a, operand, None, op), name)
                return part

            def d_scale(t, i):
                need(dve, "d_sc", t + 1)
                sig(v.tensor_scalar(d_q2[:, :], d_xn[:, :], d_s[:, 3:4], ROUND, ALU.mult, ALU.add), "d_q2")

            def d_unscale(t, i):
                need(dve, "d_q2", t + 1)
                need(dve, "d_rs", t + 1)
                need(dve, "d_T", t)
                sig(v.tensor_scalar(d_q3[:, :], d_q2[:, :], ROUND, d_s[:, 4:5], ALU.subtract, ALU.mult), "d_q3")

            def d_silu(t, i):
                need(dve, "d_th", t + 1)
                sig(v.scalar_tensor_tensor(d_g[:, :], d_th[:, :], 1.0, d1[:, :], ALU.add, ALU.mult), "d_g")

            def d_gscale(t, i):
                need(dve, "d_gsc", t + 1)
                need(dve, "d_GT", t)
                sig(v.tensor_scalar(d_g2[:, :], d_g[:, :], d_s[:, 11:12], ROUND, ALU.mult, ALU.add), "d_g2")

            def d_end(t, i):
                need(dve, "d_acc", t + 1)
                if not isinstance(t, int):
                    dve.wait_ge(y_out[i], (t - i) * 8)
                elif t > 1:
                    dve.wait_ge(y_out[i], 16 * (t // 2))
                sig(v.scalar_tensor_tensor(y[i][:, :], d1[:, 0:P], d1[:, P:P + 1], x3[i][:, :], ALU.mult, ALU.add), "d_out")

            d_clip = one(1, ALU.max, QCLIP, 0, "d_am", "d_cl")
            d_rcp = one(2, None, None, 1, "d_cl", "d_rc")
            d_127 = one(3, ALU.mult, QMAX, 2, "d_rc", "d_sc")
            d_rsc = one(4, ALU.mult, 1.0 / QMAX, 1, "d_cl", "d_rs")
            d_gclip = one(9, ALU.max, 2 * QCLIP, 8, "d_gam", "d_gcl")
            d_grcp = one(10, None, None, 9, "d_gcl", "d_grc")
            d_g127 = one(11, ALU.mult, QMAX, 10, "d_grc", "d_gsc")
            d_grsc = one(12, ALU.mult, wstat[:, 6:7], 9, "d_gcl", "d_grs", "d_acc")
            d_absmax, d_gabsmax = absmax(d_xn, 0, "d_xn", "d_am"), absmax(d_g, 8, "d_g", "d_gam")
            b_norm = norm("x1", x1, b_xn, "b_xn", ["b_T"])
            c_norm = norm("x2", x2, c_xn, "c_xn", ["c_T"])
            d_norm = norm("x3", x3, d_xn, "d_xn", ["d_q2"])
            a_norm = norm("x", xin, a_xn, "a_xn", ["a_T"])
            c_max0, c_max1 = c_maxes(0, c0), c_maxes(1, c1)
            bn_x, bn_x1, bn_x2, bn_x3 = bn("x", xin), bn("x1", x1), bn("x2", x2), bn("x3", x3)
            aggr_x, aggr_x1, aggr_x2, aggr_x3 = (aggr(s) for s in stat)
            vareps_x, vareps_x1, vareps_x2, vareps_x3 = (vareps(s) for s in stat)
            run(dve, [
                (4, c_max0), (5, d_rsc), (0, bn_x), (5, d_unscale), (2, b_maxes), (4, c_max1), (1, a_recip),
                (0, aggr_x), (0, vareps_x), (3, z_sum1), (3, z_sum2), (3, z_sum3), (2, b_vsum1), (0, a_norm),
                (3, z_end), (1, a_end), (2, b_vsum3), (1, bn_x1), (4, c_recips), (1, aggr_x1), (3, bn_x2),
                (1, vareps_x1), (4, c_normalise), (3, aggr_x2), (5, d_silu), (3, vareps_x2), (5, d_gabsmax),
                (3, c_norm), (4, c_end), (4, bn_x3), (1, b_norm), (5, d_gclip), (2, b_recips), (4, aggr_x3),
                (5, d_grcp), (5, d_g127), (5, d_gscale), (4, vareps_x3), (5, d_grsc), (4, d_norm),
                (4, d_absmax), (4, d_clip), (4, d_rcp), (1, b_compare), (4, d_127), (2, b_coef), (1, b_ranks),
                (4, d_scale), (0, a_max), (5, d_end), (1, b_masks), (1, b_vgates)])


def kernel(**inputs):
    import numpy as np
    import concourse.bacc as bacc
    from concourse.bass_utils import run_bass_kernel_spmd as run_spmd

    nc = bacc.Bacc("TRN2", target_bir_lowering=False, num_devices=1)
    arrays = {}

    def give(name, a):
        a = np.ascontiguousarray(a)
        arrays[name] = a
        return nc.dram_tensor(name, a.shape, mybir.dt.from_np(a.dtype), kind="ExternalInput").ap()

    g = {n: np.asarray(a) for n, a in inputs.items()}
    column, row = (lambda a: a.reshape(-1, 1)), (lambda a: a.reshape(1, -1))
    w = {
        "a_wqT": g["L0_xattn_Wq"].T, "a_wkT": g["L0_xattn_Wk"].T, "a_wvT": g["L0_xattn_Wv"].T,
        "a_bq": column(g["L0_xattn_bq"]), "a_bk": column(g["L0_xattn_bk"]), "a_bv": row(g["L0_xattn_bv"]),
        "m_wq": g["L0_ffn_Wq"], "m_wk": g["L0_ffn_Wk"], "m_ws": g["L0_ffn_Ws"], "m_wd": g["L0_ffn_Wd"],
        "m_wv": g["L0_ffn_Wv"], "m_wo": g["L0_ffn_Wo"],
        "c_wqT": g["L1_xattn_Wq"].T, "c_wkT": g["L1_xattn_Wk"].T, "c_wvT": g["L1_xattn_Wv"].T,
        "c_bq": column(g["L1_xattn_bq"]), "c_bk": column(g["L1_xattn_bk"]), "c_bv": column(g["L1_xattn_bv"]),
        "c_woT": g["L1_xattn_Wo"].T, "c_bo": row(g["L1_xattn_bo"]),
        "w1": g["L1_ffn_w1"], "convw": g["L1_ffn_conv_w"], "convb": row(g["L1_ffn_conv_b"]), "w2": g["L1_ffn_w2"],
    }
    jmask = np.zeros((P, J1), np.float32)
    batch = np.zeros((2, 2, P), np.float32)
    alt = np.zeros((P, P), np.float32)
    for p in range(P):
        jmask[p, p // HD % J1] = 1.0
        batch[p // SEQ, 0, p] = 1.0
        alt[p, 2 * (p % SEQ) + p // SEQ] = 1.0
        batch[1 - p // SEQ, 1, p] = CROSS
    x = give("x_dram", g["x"])
    ctx1024 = give("ctx_dram", g["ctx_1024"])
    mask = give("mask_dram", g["mask_BxS2_bf1"])
    w = {n: give(n + "_dram", a) for n, a in w.items()}
    consts = {"ident": give("ident_dram", np.eye(P, dtype=np.float32)), "jmask": give("jmask_dram", jmask),
              "alt": give("alt_dram", alt), "altT": give("altT_dram", alt.T),
              "batch": give("batch_dram", batch)}
    out = nc.dram_tensor("out_dram", (NB, SEQ, D), F32, kind="ExternalOutput").ap()
    moe_transformer(nc, x, ctx1024, mask, w, consts, out)
    return run_spmd(nc, [arrays], core_ids=[0]).results[0]["out_dram"]
```
